# Optimizing a Trainium2 kernel written in Bass

```python
import numpy as np
import jax
import jax.numpy as jnp

def _softmax(x, axis=-1):
    return jax.nn.softmax(x, axis=axis)

def _gelu(x):
    return jax.nn.gelu(x, approximate=True)

def _silu(x):
    return jax.nn.silu(x)

def _sigmoid(x):
    return jax.nn.sigmoid(x)

def _layernorm(x, axis=-1, eps=1e-05):
    m = jnp.mean(x, axis=axis, keepdims=True)
    v = jnp.var(x, axis=axis, keepdims=True)
    return (x - m) / jnp.sqrt(v + eps)

def _scatter_add(tgt, idx, src, axis=0):
    return tgt.at[idx].add(src)

def _segment_sum(src, seg, n):
    return jax.ops.segment_sum(src, seg, n)
kernel_name = 'mk_vit_tower_d1_tok_img768_r4_48a25b'

def setup_inputs(seed: int=0):
    np.random.seed(seed)
    _w = jnp.asarray

    def _rec_inputs():
        import jax
        import jax.numpy as jnp
        _rk = jax.random.key(seed)
        x = -0.000222058 + 0.999998 * jax.random.normal(jax.random.fold_in(_rk, 1), (64, 3, 96, 96), jnp.float32)
        return x
    x = _rec_inputs()

    def _L0_tok_setup():
        import jax, jax.numpy as jnp
        import numpy as np
        from jax import lax
        HIDDEN = 192
        C_IN = 3
        PATCH = 16
        SIDE = 32
        NUM_PATCHES = SIDE * SIDE

        def _position_ids(nb_h, nb_w):
            boundaries = np.arange(1.0 / SIDE, 1.0, 1.0 / SIDE, dtype=np.float32)
            frac_h = np.arange(0.0, 1.0 - 1e-06, 1.0 / nb_h, dtype=np.float32)
            frac_w = np.arange(0.0, 1.0 - 1e-06, 1.0 / nb_w, dtype=np.float32)
            bh = np.searchsorted(boundaries, frac_h, side='right')
            bw = np.searchsorted(boundaries, frac_w, side='right')
            return jnp.asarray((bh[:, None] * SIDE + bw).reshape(-1), dtype=jnp.int32)
        key = jax.random.key(seed)
        k1, k2, k3 = jax.random.split(key, 3)
        pixel_values = jax.random.normal(k1, (32, C_IN, 128, 128), dtype=jnp.float32)
        conv_w = jax.random.normal(k2, (HIDDEN, C_IN, PATCH, PATCH), dtype=jnp.float32) * 0.02
        conv_b = jnp.zeros((HIDDEN,), dtype=jnp.float32)
        pos_table = jax.random.normal(k3, (NUM_PATCHES, HIDDEN), dtype=jnp.float32) * 0.02
        return {'pixel_values': pixel_values, 'conv_w': conv_w, 'conv_b': conv_b, 'pos_table': pos_table}
    _L0_tok_all = _L0_tok_setup()
    _L0_tok_in = {k: v for k, v in _L0_tok_all.items() if k in ('conv_w', 'conv_b', 'pos_table')}
    del _L0_tok_all

    def _L0_attn_setup():
        import jax, jax.numpy as jnp
        import numpy as np
        NHEAD = 12
        EPS = 1e-05

        def layernorm_nobias(x, gamma):
            mu = jnp.mean(x, axis=-1, keepdims=True)
            var = jnp.var(x, axis=-1, keepdims=True)
            return (x - mu) * jax.lax.rsqrt(var + EPS) * gamma
        key = jax.random.key(seed)
        ks = jax.random.split(key, 10)
        b, l, d = (4, 512, 192)
        s = d ** (-0.5)
        return {'x': jax.random.normal(ks[0], (b, l, d), jnp.float32), 'Wq': jax.random.normal(ks[1], (d, d), jnp.float32) * s, 'Wk': jax.random.normal(ks[2], (d, d), jnp.float32) * s, 'bk': jax.random.normal(ks[3], (d,), jnp.float32) * 0.02, 'Wv': jax.random.normal(ks[4], (d, d), jnp.float32) * s, 'bv': jax.random.normal(ks[5], (d,), jnp.float32) * 0.02, 'gq': jnp.ones((d,), jnp.float32), 'gk': jnp.ones((d,), jnp.float32), 'Wo': jax.random.normal(ks[6], (d, d), jnp.float32) * s, 'bo': jnp.zeros((d,), jnp.float32)}
    _L0_attn_all = _L0_attn_setup()
    _L0_attn_in = {k: v for k, v in _L0_attn_all.items() if k in ('Wq', 'Wk', 'bk', 'Wv', 'bv', 'gq', 'gk', 'Wo', 'bo')}
    del _L0_attn_all

    def _L0_ffn_setup():
        import jax, jax.numpy as jnp
        import numpy as np
        D_MODEL = 192
        D_FF = 768
        N_EXPERTS = 9
        key = jax.random.key(seed)
        ks = jax.random.split(key, 7)
        scale = 0.02
        return {'x': jax.random.normal(ks[0], (2, 256, D_MODEL), jnp.float32), 'Ws': jax.random.normal(ks[1], (D_MODEL, N_EXPERTS), jnp.float32) * scale, 'bs': jnp.zeros((N_EXPERTS,), jnp.float32), 'W1': jax.random.normal(ks[2], (N_EXPERTS, D_MODEL, D_FF), jnp.float32) * scale, 'b1': jnp.zeros((N_EXPERTS, D_FF), jnp.float32), 'W2': jax.random.normal(ks[3], (N_EXPERTS, D_FF, D_MODEL), jnp.float32) * scale, 'b2': jnp.zeros((N_EXPERTS, D_MODEL), jnp.float32)}
    _L0_ffn_all = _L0_ffn_setup()
    _L0_ffn_in = {k: v for k, v in _L0_ffn_all.items() if k in ('Ws', 'bs', 'W1', 'b1', 'W2', 'b2')}
    del _L0_ffn_all
    return {'x': x, 'L0_tok_conv_w': _L0_tok_in['conv_w'], 'L0_tok_conv_b': _L0_tok_in['conv_b'], 'L0_tok_pos_table': _L0_tok_in['pos_table'], 'L0_attn_Wq': _L0_attn_in['Wq'], 'L0_attn_Wk': _L0_attn_in['Wk'], 'L0_attn_bk': _L0_attn_in['bk'], 'L0_attn_Wv': _L0_attn_in['Wv'], 'L0_attn_bv': _L0_attn_in['bv'], 'L0_attn_gq': _L0_attn_in['gq'], 'L0_attn_gk': _L0_attn_in['gk'], 'L0_attn_Wo': _L0_attn_in['Wo'], 'L0_attn_bo': _L0_attn_in['bo'], 'L0_ffn_Ws': _L0_ffn_in['Ws'], 'L0_ffn_bs': _L0_ffn_in['bs'], 'L0_ffn_W1': _L0_ffn_in['W1'], 'L0_ffn_b1': _L0_ffn_in['b1'], 'L0_ffn_W2': _L0_ffn_in['W2'], 'L0_ffn_b2': _L0_ffn_in['b2']}

def reference(x, L0_tok_conv_w, L0_tok_conv_b, L0_tok_pos_table, L0_attn_Wq, L0_attn_Wk, L0_attn_bk, L0_attn_Wv, L0_attn_bv, L0_attn_gq, L0_attn_gk, L0_attn_Wo, L0_attn_bo, L0_ffn_Ws, L0_ffn_bs, L0_ffn_W1, L0_ffn_b1, L0_ffn_W2, L0_ffn_b2):
    import jax
    import jax.numpy as jnp

    def _L0_tok_ref(pixel_values, conv_w, conv_b, pos_table):
        import jax, jax.numpy as jnp
        import numpy as np
        from jax import lax
        HIDDEN = 192
        C_IN = 3
        PATCH = 16
        SIDE = 32
        NUM_PATCHES = SIDE * SIDE

        def _position_ids(nb_h, nb_w):
            boundaries = np.arange(1.0 / SIDE, 1.0, 1.0 / SIDE, dtype=np.float32)
            frac_h = np.arange(0.0, 1.0 - 1e-06, 1.0 / nb_h, dtype=np.float32)
            frac_w = np.arange(0.0, 1.0 - 1e-06, 1.0 / nb_w, dtype=np.float32)
            bh = np.searchsorted(boundaries, frac_h, side='right')
            bw = np.searchsorted(boundaries, frac_w, side='right')
            return jnp.asarray((bh[:, None] * SIDE + bw).reshape(-1), dtype=jnp.int32)
        B, _, H, W = pixel_values.shape
        nb_h, nb_w = (H // PATCH, W // PATCH)
        patches = lax.conv_general_dilated(pixel_values, conv_w, window_strides=(PATCH, PATCH), padding='VALID', dimension_numbers=('NCHW', 'OIHW', 'NCHW'))
        patches = patches + conv_b[None, :, None, None]
        embeddings = patches.reshape(B, HIDDEN, nb_h * nb_w).transpose(0, 2, 1)
        pos_ids = _position_ids(nb_h, nb_w)
        pos_emb = pos_table[pos_ids]
        return embeddings + pos_emb[None, :, :]

    def _L0_attn_ref(x, Wq, Wk, bk, Wv, bv, gq, gk, Wo, bo):
        import jax, jax.numpy as jnp
        import numpy as np
        NHEAD = 12
        EPS = 1e-05

        def layernorm_nobias(x, gamma):
            mu = jnp.mean(x, axis=-1, keepdims=True)
            var = jnp.var(x, axis=-1, keepdims=True)
            return (x - mu) * jax.lax.rsqrt(var + EPS) * gamma
        b, l, d = x.shape
        n = NHEAD
        hd = d // n
        scale = hd ** (-0.5)
        q = layernorm_nobias(x @ Wq.T, gq)
        k = layernorm_nobias(x @ Wk.T + bk, gk)
        v = x @ Wv.T + bv
        q = q.reshape(b, l, n, hd).transpose(0, 2, 1, 3)
        k = k.reshape(b, l, n, hd).transpose(0, 2, 1, 3)
        v = v.reshape(b, l, n, hd).transpose(0, 2, 1, 3)
        scores = jnp.einsum('bnqd,bnkd->bnqk', q, k) * scale
        attn = jax.nn.softmax(scores, axis=-2)
        o = jnp.einsum('bnqk,bnkd->bnqd', attn, v)
        o = o.transpose(0, 2, 1, 3).reshape(b, l, d)
        return o @ Wo.T + bo + x

    def _L0_ffn_ref(x, Ws, bs, W1, b1, W2, b2):
        import jax, jax.numpy as jnp
        import numpy as np
        D_MODEL = 192
        D_FF = 768
        N_EXPERTS = 9
        B, S, d = x.shape
        xt = x.reshape(-1, d)
        route_prob = jax.nn.softmax(xt @ Ws + bs, axis=-1)
        p = jnp.max(route_prob, axis=-1)
        routes = jnp.argmax(route_prob, axis=-1)
        h = jax.nn.gelu(jnp.einsum('td,edf->tef', xt, W1) + b1, approximate=False)
        out = jnp.einsum('tef,efd->ted', h, W2) + b2
        common = out[:, 0, :]
        sel = jnp.take_along_axis(out, routes[:, None, None], axis=1)[:, 0, :]
        scaling = (p / jax.lax.stop_gradient(p))[:, None]
        pe = p[:, None]
        final = jnp.where((routes == 0)[:, None], common * scaling, pe * sel + (1.0 - pe) * common)
        return final.reshape(B, S, d)
    h = _L0_tok_ref(x, L0_tok_conv_w, L0_tok_conv_b, L0_tok_pos_table)
    h = h + _L0_attn_ref(_layernorm(h, axis=-1), L0_attn_Wq, L0_attn_Wk, L0_attn_bk, L0_attn_Wv, L0_attn_bv, L0_attn_gq, L0_attn_gk, L0_attn_Wo, L0_attn_bo)
    h = h + _L0_ffn_ref(_layernorm(h, axis=-1), L0_ffn_Ws, L0_ffn_bs, L0_ffn_W1, L0_ffn_b1, L0_ffn_W2, L0_ffn_b2)
    return h

_drawn_inputs = setup_inputs


def setup_inputs(seed=0):
    import zlib

    import numpy as np

    out = dict(_drawn_inputs(seed))
    spreads = {'L0_tok_conv_b': (0.0, 0.1),
     'L0_attn_gq': (1.0, 0.554),
     'L0_attn_gk': (1.0, 0.2),
     'L0_attn_bo': (0.0, 0.1),
     'L0_ffn_bs': (0.0, 0.8),
     'L0_ffn_b1': (0.0, 0.503),
     'L0_ffn_b2': (0.0, 0.1)}
    factors = {'L0_attn_bk': 8.0, 'L0_attn_bv': 3.746, 'L0_ffn_Ws': 4.257}
    for name, (base, spread) in spreads.items():
        noise = np.random.default_rng([zlib.crc32(name.encode()), seed]).standard_normal(out[name].shape)
        drawn = base * np.exp(spread * noise) if base else spread * noise
        out[name] = jnp.asarray(drawn.astype(out[name].dtype))
    for name, factor in factors.items():
        out[name] = (out[name] * factor).astype(out[name].dtype)
    return out
```

```python
from contextlib import ExitStack

import concourse.bass as bass
from concourse import mybir

F32 = mybir.dt.float32
I32 = mybir.dt.int32
ALU = mybir.AluOpType
ACT = mybir.ActivationFunctionType
AX = mybir.AxisListType

P = 128
IMAGES, CHANNELS, SIDE = 64, 3, 96
PATCH = 16
GRID = SIDE // PATCH
SEQ = GRID * GRID
TOKENS = IMAGES * SEQ
TILES = TOKENS // P
D = 192
DB = D - P
PIXELS = CHANNELS * PATCH * PATCH
KC = PIXELS // P
HEADS, HD = 12, 16
HEADS_A = P // HD
PAIRS = HEADS // 2
DFF = 768
FC = DFF // P
FH = DFF // 2
EXPERTS = 9
EPS = 1e-5
GROUPS = (TOKENS + EXPERTS * (P - 1)) // P
STEP_IMAGES = 2
FIRST_ROWS = 3
STEPS = IMAGES // STEP_IMAGES
STEP_TOKENS = STEP_IMAGES * SEQ
K2 = 2 * SEQ
TE = TILES * EXPERTS
POS_TABLE_SIDE = 32

CONSTS = {}
_at = 0
for _name, _n in (("ident", P), ("before", P), ("ones", P), ("first", EXPERTS), ("thresholds", TILES),
                  ("groups", GROUPS), ("keep", TE), ("heads_a", HEADS_A), ("heads_b", HEADS - HEADS_A),
                  ("parity", 2)):
    CONSTS[_name] = (_at, _at + _n)
    _at += _n
NCONST = _at


def tile_at(i, k):
    return 2 * i + k, k % 2, i + k // 2


def vit_kernel(nc, patches, conv_w, conv_b, pos, w_qkv, w_o, gq, gk, w_router, w1, w1_rest, w2, b2, consts, out):
    packed = nc.dram_tensor("packed_tokens", (GROUPS * P, D), F32, kind="Internal").ap()
    packed_y = nc.dram_tensor("packed_outputs", (GROUPS * P, D), F32, kind="Internal").ap()
    v_dram = nc.dram_tensor("v_rows", (TOKENS, D), F32, kind="Internal").ap()
    v_by_image = v_dram.rearrange("(n k) d -> k n d", k=SEQ)

    with ExitStack() as ctx:
        def sb(name, cols, dt=F32):
            return ctx.enter_context(nc.sbuf_tensor(name, [P, cols], dt))

        def sem(name):
            return ctx.enter_context(nc.semaphore(name))

        bank = [ctx.enter_context(nc.psum_tensor(f"bank{i}", [P, 512], F32)) for i in range(8)]

        W1A = sb("W1A", EXPERTS * DFF)
        W1B = sb("W1B", EXPERTS * DFF)
        W2 = sb("W2", EXPERTS * FC * D)
        B2 = sb("B2", EXPERTS * D)
        H = sb("H", TILES * D)
        QK = sb("QK", 4 * TOKENS)
        CST = sb("CST", NCONST)
        WO = sb("WO", 2 * D)
        WR = sb("WR", 2 * EXPERTS)
        NEGHALF = sb("NEGHALF", 2)
        LOG = sb("LOG", TE)
        KEEP1 = sb("KEEP1", TILES)
        SHARE = sb("SHARE", TILES)
        SLOT = sb("SLOT", TILES, I32)
        GROUP_EXPERT = sb("GROUP_EXPERT", GROUPS, I32)

        def const(name, rows=P):
            a, b = CONSTS[name]
            return CST[0:rows, a:b]

        ARENA = sb("ARENA", 5800)
        marks = [0]

        def cut(n):
            a = marks[0]
            marks[0] += n
            assert marks[0] <= 5800
            return ARENA[:, a:a + n]

        PT = [cut(KC * P) for _ in range(2)]
        CW = cut(KC * D)
        WQKV = [cut(3 * D) for _ in range(2)]
        XN = [cut(D) for _ in range(2)]
        QKN = [cut(2 * D) for _ in range(2)]
        VST = [cut(D) for _ in range(2)]
        marks[0] = 0
        HS = cut(DFF)
        HT = cut(DFF)
        XR = [cut(D) for _ in range(2)]
        YR = [cut(D) for _ in range(2)]
        OR = [cut(2 * P) for _ in range(2)]
        GR = [cut(D) for _ in range(4)]
        OUTR = [cut(D) for _ in range(4)]
        RT = cut(8 * TE)

        XT = [sb(f"XT{i}", 2 * P) for i in range(2)]
        KR = [sb(f"KR{i}", STEP_IMAGES * HEADS * SEQ) for i in range(2)]
        SB = [sb(f"SB{i}", STEP_IMAGES * PAIRS * SEQ) for i in range(2)]
        PR = [sb(f"PR{i}", STEP_IMAGES * PAIRS * SEQ) for i in range(2)]
        V2 = [sb(f"V2{i}", STEP_IMAGES * D) for i in range(2)]
        VS = [sb(f"VS{i}", STEP_IMAGES * D) for i in range(2)]
        NP2 = STEP_IMAGES * PAIRS
        MX = sb("MX", NP2)
        SM = sb("SM", NP2)
        RC = sb("RC", NP2)
        R2 = sb("R2", 2 * NP2)
        GAIN = sb("GAIN", 4)
        GM = sb("GM", HEADS)
        STH = sb("STH", 6)
        STQK = sb("STQK", 12)
        MVH = [sb(f"MVH{i}", 2) for i in range(2)]
        MVQK = [sb(f"MVQK{i}", 4) for i in range(2)]
        RSH = [sb(f"RSH{i}", 1) for i in range(2)]
        RSQK = [sb(f"RSQK{i}", 2) for i in range(2)]
        VE = sb("VE", 3)
        CB = sb("CB", D)
        SMALL = sb("SMALL", 16 * TILES)
        SMALLE = sb("SMALLE", 8 * EXPERTS)
        GCMP = sb("GCMP", GROUPS * EXPERTS)

        QA, QB = QK[:, 0:TOKENS], QK[:, TOKENS:2 * TOKENS]
        KA, KB = QK[:, 2 * TOKENS:3 * TOKENS], QK[:, 3 * TOKENS:4 * TOKENS]
        XN2 = QK[:, 2 * TOKENS:2 * TOKENS + TILES * D]
        COMMON = QK[:, 0:2 * TOKENS].rearrange("p (g n) -> p g n", g=2)

        consts_in = sem("consts_in")
        pos_in = [sem(f"pos_in{i}") for i in range(2)]
        gains_in = sem("gains_in")
        patch_w_in = sem("patch_w_in")
        mixer_w_in = sem("mixer_w_in")
        expert_w_in = sem("expert_w_in")
        patch_in = [sem(f"patch_in{i}") for i in range(2)]
        gains_ready = sem("gains_ready")
        set_up = sem("set_up")
        h_set = sem("h_set")
        conv_done = sem("conv_done")
        h_added = sem("h_added")
        h_stats = sem("h_stats")
        h_aggr = sem("h_aggr")
        h_rstd = sem("h_rstd")
        xn_ready = sem("xn_ready")
        h_plus_xn = sem("h_plus_xn")
        xt_transposed = sem("xt_transposed")
        xt_copied = sem("xt_copied")
        qk_done = sem("qk_done")
        v_done = sem("v_done")
        v_copied = sem("v_copied")
        v_stored = [sem(f"v_stored{i}") for i in range(2)]
        qk_stats = sem("qk_stats")
        qk_aggr = sem("qk_aggr")
        qk_rstd = sem("qk_rstd")
        qk_normed = sem("qk_normed")
        qkT_done = sem("qkT_done")
        qkT_copied = sem("qkT_copied")
        waited = sem("waited")
        ve_h = sem("ve_h")
        ve_qk = sem("ve_qk")
        kr_ready = sem("kr_ready")
        scores_done = sem("scores_done")
        max_ready = sem("max_ready")
        s_shifted = sem("s_shifted")
        exp_done = sem("exp_done")
        denom = sem("denom")
        v2_in = [sem(f"v2_in{i}") for i in range(2)]
        vs_ready = sem("vs_ready")
        pv_done = sem("pv_done")
        o_copied = sem("o_copied")
        or_ready = sem("or_ready")
        w_done = sem("w_done")
        h2_added = sem("h2_added")
        h2_stats = sem("h2_stats")
        h2_aggr = sem("h2_aggr")
        h2_rstd = sem("h2_rstd")
        xn2_ready = sem("xn2_ready")
        xn2_saved = sem("xn2_saved")
        ffn_t_done = sem("ffn_t_done")
        ffn_xt = sem("ffn_xt")
        f1_done = sem("f1_done")
        gelu_done = sem("gelu_done")
        ht_done = sem("ht_done")
        ht_copied = sem("ht_copied")
        y_done = sem("y_done")
        y_used = sem("y_used")
        router_done = sem("router_done")
        log_copied = sem("log_copied")
        rt = sem("rt")
        log_shifted = sem("log_shifted")
        log_exp = sem("log_exp")
        chosen = sem("chosen")
        ranks_done = sem("ranks_done")
        slots_ready = sem("slots_ready")
        groups_ready = sem("groups_ready")
        zeroed = sem("zeroed")
        packed_zeroed = sem("packed_zeroed")
        scattered = sem("scattered")
        xr_in = [sem(f"xr_in{i}") for i in range(2)]
        y_stored = [sem(f"y_stored{i}") for i in range(2)]
        gathered = [sem(f"gathered{i}") for i in range(4)]
        mixed = sem("mixed")
        out_stored = [sem(f"out_stored{i}") for i in range(4)]

        block = ctx.enter_context(nc.Block())

        def ride(e):
            e.sem_inc(waited, 1)

        def two_by_two(e, step, lags, tiles):
            last = max(lags)
            first = last + 2 + (tiles - last) % 2
            for s in range(first):
                step(0, [s - lag if s >= lag else None for lag in lags])
            with e.Fori(0, (tiles - first) // 2) as i:
                for u in range(2):
                    step(i, [first + u - lag for lag in lags])
            for s in range(tiles, tiles + last):
                step(0, [s - lag if s - lag < tiles else None for lag in lags])

        @block.sync
        def _(sp):
            def h_rows(t0, t1):
                return slice(t0 * D, t1 * D)

            sp.dma_start(PT[0], patches[0]).then_inc(patch_in[0], 16)
            sp.dma_start(CW, conv_w).then_inc(patch_w_in, 16)
            sp.dma_start(PT[1], patches[1]).then_inc(patch_in[1], 16)
            sp.dma_start(CB[:], conv_b).then_inc(pos_in[0], 16)
            sp.dma_start(H[:, h_rows(0, FIRST_ROWS)], pos[:, h_rows(0, FIRST_ROWS)]).then_inc(pos_in[0], 16)
            sp.dma_start(CST[:], consts).then_inc(consts_in, 16)
            sp.dma_start(WQKV[0], w_qkv[0:P]).then_inc(patch_w_in, 16)
            sp.dma_start(WQKV[1][0:DB + 1], w_qkv[P:D + 1]).then_inc(patch_w_in, 16)

            def load_patch(t, par):
                sp.wait_ge(conv_done, t - 1)
                sp.dma_start(PT[par], patches[bass.ds(t, 1)].rearrange("a p n -> (a p) n")).then_inc(patch_in[par], 16)

            def store_v(t, par):
                sp.wait_ge(v_copied, t + 1)
                sp.dma_start(v_dram[bass.ds(t * P, P)], VST[par]).then_inc(v_stored[par], 16)

            def load_up(e):
                cols = bass.ds(e * DFF, DFF)
                sp.dma_start(W1A[:, cols], w1[:, cols]).then_inc(expert_w_in, 16)
                sp.dma_start(W1B[0:DB + 1, cols], w1_rest[:, cols]).then_inc(expert_w_in, 16)

            def load_down(e):
                cols = bass.ds(e * FC * D, FC * D)
                sp.dma_start(W2[:, cols], w2[:, cols]).then_inc(expert_w_in, 16)

            for t in range(2, 4):
                load_patch(t, t % 2)
            sp.dma_start(H[:, h_rows(FIRST_ROWS, TILES)], pos[:, h_rows(FIRST_ROWS, TILES)]).then_inc(pos_in[1], 16)
            for row, g in enumerate((gq, gk)):
                sp.dma_start(GAIN[:, row:row + 1], g[0:P]).then_inc(gains_in, 16)
                sp.dma_start(GAIN[0:DB, 2 + row:3 + row], g[P:D]).then_inc(gains_in, 16)
            with sp.Fori(0, (TILES - 4) // 2) as i:
                for u in range(2):
                    load_patch(2 * i + 4 + u, u)
                    store_v(2 * i + u, u)
                load_up(i)
            for t in range(TILES - 4, TILES):
                store_v(t, t % 2)

            for dst, src in ((WO[:, 0:D], w_o[0:P]), (WO[0:DB + 1, D:2 * D], w_o[P:D + 1]),
                             (WR[:, 0:EXPERTS], w_router[0:P]), (WR[0:DB + 1, EXPERTS:2 * EXPERTS], w_router[P:D + 1])):
                sp.dma_start(dst, src).then_inc(mixer_w_in, 16)
            for par in range(2):
                sp.wait_ge(v_stored[par], 16 * TILES // 2)

            def v2_load(a, par):
                for copy in range(2):
                    sp.dma_start(V2[par][copy * SEQ:copy * SEQ + SEQ, :].rearrange("p (n d) -> p n d", n=STEP_IMAGES),
                                 v_by_image[:, bass.ds(a * STEP_IMAGES, STEP_IMAGES), :]).then_inc(v2_in[par], 16)

            for a in range(2):
                v2_load(a, a)
            for e in range((TILES - 4) // 2, EXPERTS):
                load_up(e)
            sp.dma_start(B2[:], b2).then_inc(expert_w_in, 16)

            def v2_next(i):
                for u in range(2):
                    a = 2 * i + 2 + u
                    sp.wait_ge(vs_ready, a - 1)
                    v2_load(a, u)

            with sp.Fori(0, EXPERTS) as i:
                v2_next(i)
                load_down(i)
            with sp.Fori(EXPERTS, (STEPS - 2) // 2) as i:
                v2_next(i)

            sp.wait_ge(scattered, 16 * TILES)
            for r in range(2):
                sp.dma_start(XR[r], packed[r * P:r * P + P]).then_inc(xr_in[r], 16)
            with sp.Fori(0, (GROUPS - 2) // 2) as i:
                for u in range(2):
                    sp.wait_ge(ffn_t_done, TILES + 2 * i + u + 1)
                    sp.dma_start(XR[u], packed[bass.ds((2 * i + u + 2) * P, P)]).then_inc(xr_in[u], 16)
                    sp.wait_ge(y_used, TILES + 2 * i + u + 1)
                    sp.dma_start(packed_y[bass.ds((2 * i + u) * P, P)], YR[u]).then_inc(y_stored[u], 16)
            for r in range(GROUPS - 2, GROUPS):
                sp.wait_ge(y_used, TILES + r + 1)
                sp.dma_start(packed_y[r * P:r * P + P], YR[r % 2]).then_inc(y_stored[r % 2], 16)
            for t in range(TILES):
                sp.wait_ge(mixed, t + 1)
                sp.dma_start(out[t * P:t * P + P], OUTR[t % 4]).then_inc(out_stored[t % 4], 16)
            for ring in range(4):
                sp.wait_ge(out_stored[ring], 16 * len(range(ring, TILES, 4)))

        @block.tensor
        def _(pe):
            ident = const("ident")

            def conv(i, k):
                t, par, half = tile_at(i, k)
                pe.wait_ge(patch_in[par], 16 * (half + 1))
                if k >= 2:
                    pe.wait_ge(h_added, t - 1)
                for c in range(KC):
                    last = pe.matmul(bank[par][:, 0:D], PT[par][:, c * P:c * P + P], CW[:, c * D:c * D + D],
                                     start=c == 0, stop=c == KC - 1)
                last.then_inc(conv_done, 1)

            def transpose_tile(src, dst):
                pe.transpose(dst[:, 0:P], src[:, 0:P], ident)
                return pe.transpose(dst[0:DB, P:2 * P], src[:, P:D], ident)

            def transpose_xn(i, k):
                t, par, half = tile_at(i, k)
                pe.wait_ge(xn_ready, t + 1)
                if k >= 1:
                    pe.wait_ge(xt_copied, t)
                transpose_tile(XN[par], bank[2]).then_inc(xt_transposed, 1)

            def project(i, k):
                t, par, half = tile_at(i, k)
                pe.wait_ge(xt_copied, t + 1)
                if k >= 2:
                    pe.wait_ge(qk_normed, t - 1)
                x = XT[par]
                pe.matmul(bank[3 + par][:, 0:2 * D], x[:, 0:P], WQKV[0][:, 0:2 * D], start=True, stop=False)
                pe.matmul(bank[3 + par][:, 0:2 * D], x[0:DB + 1, P:2 * P], WQKV[1][0:DB + 1, 0:2 * D], start=False, stop=True).then_inc(qk_done, 1)
                if k >= 1:
                    pe.wait_ge(v_copied, t)
                pe.matmul(bank[5][:, 0:D], x[:, 0:P], WQKV[0][:, 2 * D:3 * D], start=True, stop=False)
                pe.matmul(bank[5][:, 0:D], x[0:DB + 1, P:2 * P], WQKV[1][0:DB + 1, 2 * D:3 * D], start=False, stop=True).then_inc(v_done, 1)

            def transpose_qk(i, k):
                t, par, half = tile_at(i, k)
                pe.wait_ge(qk_normed, t + 1)
                pe.wait_ge(qkT_copied, t + 1)
                n = QKN[par]
                for j in range(2):
                    pe.transpose(bank[6][:, j * P:j * P + P], n[:, j * D:j * D + P], ident)
                for j in range(2):
                    last = pe.transpose(bank[6][0:DB, (2 + j) * P:(3 + j) * P], n[:, j * D + P:j * D + D], ident)
                last.then_inc(qkT_done, 1)

            def patch_step(i, ks):
                for stage, k in zip((conv, transpose_qk, project, transpose_xn), ks):
                    if k is not None:
                        stage(i, k)

            pe.sem_inc(qkT_done, 2)
            pe.wait_ge(consts_in, 16)
            pe.wait_ge(patch_w_in, 48)
            pe.wait_ge(set_up, 2)
            two_by_two(pe, patch_step, (0, 4, 2, 1), TILES)

            def scores(i, k):
                a, par, half = tile_at(i, k)
                pe.wait_ge(kr_ready, a + 1)
                if k >= 2:
                    pe.wait_ge(s_shifted, a - 1)
                ka = KR[par][:, 0:STEP_IMAGES * HEADS_A * SEQ]
                kb = KR[par][0:DB, STEP_IMAGES * HEADS_A * SEQ:]
                for n in range(STEP_IMAGES):
                    for j in range(PAIRS):
                        if j < HEADS_A // 2:
                            at = n * HEADS_A * SEQ + j * K2
                            keys, queries = ka[:, at:at + K2], QA[:, bass.ds(a * STEP_TOKENS + n * SEQ, SEQ)]
                        else:
                            at = n * (HEADS - HEADS_A) * SEQ + (j - HEADS_A // 2) * K2
                            keys, queries = kb[:, at:at + K2], QB[0:DB, bass.ds(a * STEP_TOKENS + n * SEQ, SEQ)]
                        o = (n * PAIRS + j) * SEQ
                        last = pe.matmul(bank[par][0:K2, o:o + SEQ], keys, queries, start=True, stop=True)
                last.then_inc(scores_done, 1)

            def weigh_v(i, k):
                a, par, half = tile_at(i, k)
                pe.wait_ge(vs_ready, a + 1)
                pe.wait_ge(o_copied, a + 1)
                for n in range(STEP_IMAGES):
                    for j in range(PAIRS):
                        at = n * PAIRS + j
                        row = 32 * (j % 4)
                        col = (j // 4) * STEP_TOKENS + n * SEQ
                        last = pe.matmul(bank[2 + par][row:row + 32, col:col + SEQ], VS[par][0:K2, at * 32:at * 32 + 32],
                                         PR[par][0:K2, at * SEQ:at * SEQ + SEQ], start=True, stop=True)
                last.then_inc(pv_done, 1)

            def attention_step(i, ks):
                for stage, k in zip((scores, weigh_v), ks):
                    if k is not None:
                        stage(i, k)

            pe.wait_ge(qkT_copied, TILES + 1)
            pe.wait_ge(v_copied, TILES)
            pe.wait_ge(h_added, TILES)
            two_by_two(pe, attention_step, (0, 2), STEPS)

            def project_o(i, k):
                t, par, half = tile_at(i, k)
                pe.wait_ge(or_ready, t + 1)
                if k >= 1:
                    pe.wait_ge(h2_added, t)
                o = OR[par]
                pe.matmul(bank[0][:, 0:D], o[:, 0:P], WO[:, 0:D], start=True, stop=False)
                pe.matmul(bank[0][:, 0:D], o[0:DB + 1, P:2 * P], WO[0:DB + 1, D:2 * D], start=False, stop=True).then_inc(w_done, 1)

            def ffn_transpose(n, par, guard):
                if guard:
                    pe.wait_ge(ffn_xt, n)
                transpose_tile(XR[par], bank[1]).then_inc(ffn_t_done, 1)

            def ffn_up(n, par, expert, guard):
                pe.wait_ge(ffn_xt, n + 1)
                x = XT[par]
                for g in range(2):
                    if guard:
                        pe.wait_ge(gelu_done, 2 * n - 1 + g)
                    pe.matmul(bank[2 + g][:, 0:FH], x[:, 0:P], W1A[:, bass.ds(expert * DFF + g * FH, FH)], start=True, stop=False)
                    pe.matmul(bank[2 + g][:, 0:FH], x[0:DB + 1, P:2 * P], W1B[0:DB + 1, bass.ds(expert * DFF + g * FH, FH)],
                              start=False, stop=True).then_inc(f1_done, 1)

            def ffn_turn(n, guard):
                if guard:
                    pe.wait_ge(ht_copied, n)
                for g in range(2):
                    pe.wait_ge(gelu_done, 2 * n + 1 + g)
                    for c in range(FC // 2):
                        last = pe.transpose(bank[4 + g][:, c * P:c * P + P], HS[:, g * FH + c * P:g * FH + c * P + P], ident)
                    last.then_inc(ht_done, 1)

            def ffn_down(n, expert, guard):
                pe.wait_ge(ht_copied, n + 1)
                if guard:
                    pe.wait_ge(y_used, n)
                for c in range(FC):
                    last = pe.matmul(bank[6][:, 0:D], HT[:, c * P:c * P + P], W2[:, bass.ds((expert * FC + c) * D, D)],
                                     start=c == 0, stop=c == FC - 1)
                last.then_inc(y_done, 1)

            def route(t, par, guard):
                if guard:
                    pe.wait_ge(log_copied, t)
                x = XT[par]
                pe.matmul(bank[7][:, 0:EXPERTS], x[:, 0:P], WR[:, 0:EXPERTS], start=True, stop=False)
                pe.matmul(bank[7][:, 0:EXPERTS], x[0:DB + 1, P:2 * P], WR[0:DB + 1, EXPERTS:2 * EXPERTS],
                          start=False, stop=True).then_inc(router_done, 1)

            def mixer_step(i, ks):
                kw, kt, kf, kh = ks
                if kh is not None:
                    ffn_turn(tile_at(i, kh)[0], kh >= 1)
                if kf is not None:
                    t, par, half = tile_at(i, kf)
                    ffn_up(t, par, 0, kf >= 1)
                    route(t, par, kf >= 1)
                if kw is not None:
                    project_o(i, kw)
                if kh is not None:
                    ffn_down(tile_at(i, kh)[0], 0, kh >= 1)
                if kt is not None:
                    t, par, half = tile_at(i, kt)
                    pe.wait_ge(xn2_ready, t + 1)
                    ffn_transpose(t, par, kt >= 1)

            pe.wait_ge(o_copied, STEPS + 2)
            pe.wait_ge(mixer_w_in, 16 * 4)
            pe.wait_ge(expert_w_in, 16 * (3 * EXPERTS + 1))
            two_by_two(pe, mixer_step, (0, 1, 2, 3), TILES)

            pe.wait_ge(chosen, 1)
            onehot = RT[:, 0:TE]
            pe.wait_ge(h2_added, TILES)
            pe.matmul(bank[0][:, 0:TE], const("before"), onehot, start=True, stop=True)
            pe.matmul(bank[7][:, 0:TE], const("ones"), onehot, start=True, stop=True).then_inc(ranks_done, 1)

            def group_step(i, ks):
                kt, kf, kh = ks
                if kh is not None:
                    n, par, half = tile_at(i, kh)
                    ffn_turn(TILES + n, True)
                if kf is not None:
                    n, par, half = tile_at(i, kf)
                    expert = pe.value_load(GROUP_EXPERT[0:1, bass.ds(n, 1)], min_val=0, max_val=EXPERTS - 1)
                    ffn_up(TILES + n, par, expert, True)
                if kh is not None:
                    n, par, half = tile_at(i, kh)
                    expert = pe.value_load(GROUP_EXPERT[0:1, bass.ds(n, 1)], min_val=0, max_val=EXPERTS - 1)
                    ffn_down(TILES + n, expert, True)
                if kt is not None:
                    n, par, half = tile_at(i, kt)
                    pe.wait_ge(xr_in[par], 16 * (half + 1))
                    ffn_transpose(TILES + n, par, True)

            pe.wait_ge(groups_ready, 1)
            two_by_two(pe, group_step, (0, 1, 2), GROUPS)

        @block.scalar
        def _(act):
            def copy_xt(src, par):
                act.activation(XT[par][:, 0:P], src[:, 0:P], ACT.Copy)
                return act.activation(XT[par][0:DB, P:2 * P], src[0:DB, P:2 * P], ACT.Copy)

            def patch_step(i, ks):
                kx, kv, kq = ks
                if kx is not None:
                    t, par, half = tile_at(i, kx)
                    act.wait_ge(xt_transposed, t + 1)
                    if kx >= 2:
                        act.wait_ge(v_done, t - 1)
                    copy_xt(bank[2], par).then_inc(xt_copied, 1)
                if kv is not None:
                    t, par, half = tile_at(i, kv)
                    act.wait_ge(v_done, t + 1)
                    if kv >= 2:
                        act.wait_ge(v_stored[par], 16 * half)
                    act.activation(VST[par], bank[5][:, 0:D], ACT.Copy).then_inc(v_copied, 1)
                if kq is not None:
                    t, par, half = tile_at(i, kq)
                    act.wait_ge(qkT_done, t + 3)
                    qk = QK[:, :].rearrange("p (j g n) -> p j g n", j=2, g=2)
                    act.activation(qk[:, :, 0, bass.ds(t * P, P)],
                                   bank[6][:, 0:2 * P].rearrange("p (j n) -> p j n", j=2), ACT.Copy)
                    act.activation(qk[0:DB, :, 1, bass.ds(t * P, P)],
                                   bank[6][0:DB, 2 * P:4 * P].rearrange("p (j n) -> p j n", j=2), ACT.Copy).then_inc(qkT_copied, 1)

            act.sem_inc(qkT_copied, 1)
            act.sem_inc(o_copied, 2)
            two_by_two(act, patch_step, (1, 2, 4), TILES)

            def attention_step(i, ks):
                ke, ko = ks
                if ke is not None:
                    a, par, half = tile_at(i, ke)
                    act.wait_ge(s_shifted, a + 1)
                    if ke >= 2:
                        act.wait_ge(pv_done, a - 1)
                    act.activation(PR[par][0:K2, :], SB[par][0:K2, :], ACT.Exp, scale=HD ** -0.5).then_inc(exp_done, 1)
                if ko is not None:
                    a, par, half = tile_at(i, ko)
                    act.wait_ge(pv_done, a + 1)
                    act.activation(QA[:, bass.ds(a * STEP_TOKENS, STEP_TOKENS)], bank[2 + par][:, 0:STEP_TOKENS], ACT.Copy)
                    act.activation(QB[0:DB, bass.ds(a * STEP_TOKENS, STEP_TOKENS)],
                                   bank[2 + par][0:DB, STEP_TOKENS:2 * STEP_TOKENS], ACT.Copy).then_inc(o_copied, 1)

            two_by_two(act, attention_step, (0, 2), STEPS)

            def gelu(n, guard):
                for g in range(2):
                    act.wait_ge(f1_done, 2 * n + 1 + g)
                    if guard and g == 0:
                        act.wait_ge(ht_done, 2 * n)
                    act.activation(HS[:, g * FH:g * FH + FH], bank[2 + g][:, 0:FH], ACT.Gelu).then_inc(gelu_done, 1)

            def mixer_step(i, ks):
                ko, kx, kg = ks
                if ko is not None:
                    t, par, half = tile_at(i, ko)
                    if ko >= 2:
                        act.wait_ge(w_done, t - 1)
                    act.activation(OR[par][:, 0:P], QA[:, bass.ds(t * P, P)], ACT.Copy)
                    act.activation(OR[par][0:DB, P:2 * P], QB[0:DB, bass.ds(t * P, P)], ACT.Copy).then_inc(or_ready, 1)
                if kg is not None:
                    gelu(tile_at(i, kg)[0], kg >= 1)
                if kx is not None:
                    t, par, half = tile_at(i, kx)
                    act.wait_ge(ffn_t_done, t + 1)
                    if kx >= 2:
                        act.wait_ge(router_done, t - 1)
                    copy_xt(bank[1], par).then_inc(ffn_xt, 1)

            act.wait_ge(o_copied, STEPS + 2)
            act.wait_ge(set_up, 4)
            two_by_two(act, mixer_step, (0, 1, 2), TILES)

            act.wait_ge(log_shifted, 1)
            act.activation(RT[:, 3 * TE:4 * TE], RT[:, 2 * TE:3 * TE], ACT.Exp).then_inc(log_exp, 1)

            def group_step(i, ks):
                kx, kg = ks
                if kg is not None:
                    gelu(TILES + tile_at(i, kg)[0], True)
                if kx is not None:
                    n, par, half = tile_at(i, kx)
                    act.wait_ge(ffn_t_done, TILES + n + 1)
                    act.wait_ge(f1_done, 2 * (TILES + n - 1))
                    copy_xt(bank[1], par).then_inc(ffn_xt, 1)

            two_by_two(act, group_step, (0, 1), GROUPS)

        @block.vector
        def _(dve):
            def norm(dst, src, mv, rstd):
                return dve.tensor_scalar(dst, src, mv[:, 0:1], rstd, ALU.subtract, ALU.mult)

            for par in range(2):
                dve.memset(XT[par][DB:DB + 1, P:2 * P], 1.0).then_inc(set_up, 1)
            dve.wait_ge(consts_in, 16)
            dve.wait_ge(gains_in, 64)
            dve.tensor_scalar(GM[:, 0:HEADS_A], const("heads_a"), GAIN[:, 0:1], GAIN[:, 1:2], ALU.mult, ALU.mult)
            dve.tensor_scalar(GM[0:DB, HEADS_A:HEADS], const("heads_b", DB), GAIN[0:DB, 2:3], GAIN[0:DB, 3:4],
                              ALU.mult, ALU.mult).then_inc(gains_ready, 1)
            dve.wait_ge(h_set, 1)

            def patch_step(i, ks):
                kh, kn, ks_, kq = ks
                if kn is not None:
                    t, par, half = tile_at(i, kn)
                    dve.wait_ge(h_rstd, t + 1)
                    if kn >= 2:
                        dve.wait_ge(xt_transposed, t - 1)
                        dve.wait_ge(h_plus_xn, t - 1)
                    norm(XN[par], H[:, bass.ds(t * D, D)], MVH[par], RSH[par][:, 0:1]).then_inc(xn_ready, 1)
                if kq is not None:
                    t, par, half = tile_at(i, kq)
                    dve.wait_ge(qk_rstd, t + 1)
                    dve.wait_ge(qkT_done, t + 1)
                    norm(QKN[par][:, 0:D], bank[3 + par][:, 0:D], MVQK[par][:, 0:2], RSQK[par][:, 0:1])
                    norm(QKN[par][:, D:2 * D], bank[3 + par][:, D:2 * D], MVQK[par][:, 2:4], RSQK[par][:, 1:2]).then_inc(qk_normed, 1)
                if kh is not None:
                    t, par, half = tile_at(i, kh)
                    if kh == FIRST_ROWS:
                        dve.wait_ge(h_set, 2)
                    dve.wait_ge(conv_done, t + 1)
                    h = H[:, bass.ds(t * D, D)]
                    dve.tensor_tensor(h, bank[par][:, 0:D], h, ALU.add).then_inc(h_added, 1)
                if ks_ is not None:
                    t, par, half = tile_at(i, ks_)
                    dve.wait_ge(qk_done, t + 1)
                    for j in range(2):
                        last = dve.bn_stats(STQK[:, 6 * j:6 * j + 6], bank[3 + par][:, j * D:j * D + D])
                    last.then_inc(qk_stats, 1)
                if kh is not None:
                    t, par, half = tile_at(i, kh)
                    dve.wait_ge(h_added, t + 1)
                    ride(dve)
                    dve.bn_stats(STH[:, :], H[:, bass.ds(t * D, D)]).then_inc(h_stats, 1)
                if ks_ is not None:
                    t, par, half = tile_at(i, ks_)
                    dve.wait_ge(qk_stats, t + 1)
                    ride(dve)
                    for j in range(2):
                        last = dve.bn_aggr(MVQK[par][:, 2 * j:2 * j + 2], STQK[:, 6 * j:6 * j + 6])
                    last.then_inc(qk_aggr, 1)
                if kh is not None:
                    t, par, half = tile_at(i, kh)
                    dve.wait_ge(h_stats, t + 1)
                    ride(dve)
                    dve.bn_aggr(MVH[par][:, :], STH[:, :]).then_inc(h_aggr, 1)

            two_by_two(dve, patch_step, (0, 1, 2, 4), TILES)

            def attention_step(i, ks):
                km, kd = ks
                if kd is not None:
                    a, par, half = tile_at(i, kd)
                    dve.wait_ge(exp_done, a + 1)
                    dve.reduce_sum(SM[0:K2, :], PR[par][0:K2, :].rearrange("p (m q) -> p m q", q=SEQ), axis=AX.X).then_inc(denom, 1)
                if km is not None:
                    a, par, half = tile_at(i, km)
                    dve.wait_ge(scores_done, a + 1)
                    dve.reduce_max(MX[0:K2, :], bank[par][0:K2, 0:NP2 * SEQ].rearrange("p (m q) -> p m q", q=SEQ), axis=AX.X).then_inc(max_ready, 1)
                if kd is not None:
                    dve.wait_ge(denom, 3 * tile_at(i, kd)[0] + 1)
                    dve.reciprocal(RC[0:K2, :], SM[0:K2, :]).then_inc(denom, 1)
                if km is not None:
                    a, par, half = tile_at(i, km)
                    dve.wait_ge(max_ready, a + 1)
                    dve.tensor_tensor(SB[par][0:K2, :].rearrange("p (m q) -> p m q", q=SEQ),
                                      bank[par][0:K2, 0:NP2 * SEQ].rearrange("p (m q) -> p m q", q=SEQ),
                                      MX[0:K2, :].unsqueeze(2).to_broadcast([K2, NP2, SEQ]), ALU.subtract).then_inc(s_shifted, 1)
                if kd is not None:
                    a, par, half = tile_at(i, kd)
                    dve.wait_ge(denom, 3 * a + 2)
                    dve.tensor_tensor(R2[0:K2, :].rearrange("p (m h) -> p m h", h=2),
                                      RC[0:K2, :].unsqueeze(2).to_broadcast([K2, NP2, 2]),
                                      const("parity", K2).unsqueeze(1).to_broadcast([K2, NP2, 2]), ALU.mult).then_inc(denom, 1)
                    dve.wait_ge(denom, 3 * a + 3)
                    dve.wait_ge(v2_in[par], 32 * (half + 1))
                    dve.tensor_tensor(VS[par][0:K2, :].rearrange("p (m d) -> p m d", d=HD),
                                      V2[par][0:K2, :].rearrange("p (m d) -> p m d", d=HD),
                                      R2[0:K2, :].unsqueeze(2).to_broadcast([K2, 2 * NP2, HD]), ALU.mult).then_inc(vs_ready, 1)

            two_by_two(dve, attention_step, (0, 1), STEPS)

            def take_ht(n, guard):
                if guard:
                    dve.wait_ge(y_done, n)
                for g in range(2):
                    dve.wait_ge(ht_done, 2 * n + 1 + g)
                    last = dve.tensor_copy(HT[:, g * FH:g * FH + FH], bank[4 + g][:, 0:FH])
                last.then_inc(ht_copied, 1)

            def mixer_step(i, ks):
                kw, kn, kl, kh = ks
                if kh is not None:
                    take_ht(tile_at(i, kh)[0], kh >= 1)
                if kn is not None:
                    t, par, half = tile_at(i, kn)
                    dve.wait_ge(h2_rstd, t + 1)
                    if kn >= 2:
                        dve.wait_ge(ffn_t_done, t - 1)
                        dve.wait_ge(xn2_saved, t - 1)
                    norm(XR[par], H[:, bass.ds(t * D, D)], MVH[par], RSH[par][:, 0:1]).then_inc(xn2_ready, 1)
                if kl is not None:
                    t, par, half = tile_at(i, kl)
                    dve.wait_ge(router_done, t + 1)
                    dve.tensor_copy(LOG[:, bass.ds(t * EXPERTS, EXPERTS)], bank[7][:, 0:EXPERTS]).then_inc(log_copied, 1)
                if kw is not None:
                    t, par, half = tile_at(i, kw)
                    dve.wait_ge(w_done, t + 1)
                    h = H[:, bass.ds(t * D, D)]
                    dve.tensor_tensor(h, bank[0][:, 0:D], h, ALU.add).then_inc(h2_added, 1)
                    dve.wait_ge(h2_added, t + 1)
                    ride(dve)
                    dve.bn_stats(STH[:, :], h).then_inc(h2_stats, 1)
                    dve.wait_ge(h2_stats, t + 1)
                    ride(dve)
                    dve.bn_aggr(MVH[par][:, :], STH[:, :]).then_inc(h2_aggr, 1)
                if kh is not None:
                    t, par, half = tile_at(i, kh)
                    dve.wait_ge(y_done, t + 1)
                    dve.tensor_tensor(COMMON[:, :, bass.ds(t * (D // 2), D // 2)],
                                      bank[6][:, 0:D].rearrange("p (g n) -> p g n", g=2),
                                      B2[:, 0:D].rearrange("p (g n) -> p g n", g=2), ALU.add).then_inc(y_used, 1)

            dve.wait_ge(h_plus_xn, TILES)
            for par in range(2):
                dve.memset(OR[par][DB:DB + 1, P:2 * P], 1.0).then_inc(set_up, 1)
            two_by_two(dve, mixer_step, (0, 1, 2, 3), TILES)

            steps = [0]

            def then(ins):
                steps[0] += 1
                ins.then_inc(rt, 1)
                dve.wait_ge(rt, steps[0])

            def te(n):
                return RT[:, n * TE:n * TE + TE]

            def by_tile(ap):
                return ap.rearrange("p (t e) -> p t e", e=EXPERTS)

            def by_expert(ap):
                return ap.rearrange("p (e t) -> p e t", t=TILES)

            def over_e(ap):
                return ap.unsqueeze(2).to_broadcast([P, TILES, EXPERTS])

            def over_t(ap):
                return ap.unsqueeze(1).to_broadcast([P, TILES, EXPERTS])

            def small(n):
                return SMALL[:, n * TILES:n * TILES + TILES]

            def per_e(n):
                return SMALLE[:, n * EXPERTS:n * EXPERTS + EXPERTS]

            onehot, scratch, shifted, exped = te(0), te(1), te(2), te(3)
            top, total, prob, inverse, is0, keep, pick = (small(n) for n in range(7))
            dve.wait_ge(log_copied, TILES)
            then(dve.reduce_max(top, by_tile(LOG[:, :]), axis=AX.X))
            dve.tensor_tensor(by_tile(shifted), by_tile(LOG[:, :]), over_e(top), ALU.subtract).then_inc(log_shifted, 1)
            then(dve.tensor_tensor(by_tile(scratch), by_tile(LOG[:, :]), over_e(top), ALU.is_equal))
            then(dve.tensor_tensor(by_tile(scratch), by_tile(scratch), over_t(const("first")), ALU.mult))
            then(dve.reduce_max(pick, by_tile(scratch), axis=AX.X))
            dve.tensor_tensor(by_tile(onehot), over_t(const("first")), over_e(pick), ALU.is_equal).then_inc(chosen, 1)
            dve.wait_ge(log_exp, 1)
            then(dve.reduce_sum(total, by_tile(exped), axis=AX.X))
            then(dve.reciprocal(prob, total))
            then(dve.reciprocal(inverse, prob))
            dve.tensor_copy(is0, by_tile(onehot)[:, :, 0])
            then(dve.tensor_tensor(inverse, prob, inverse, ALU.mult))
            then(dve.tensor_scalar(keep, prob, -1.0, 1.0, ALU.mult, ALU.add))
            then(dve.tensor_tensor(inverse, inverse, keep, ALU.subtract))
            then(dve.tensor_tensor(inverse, inverse, is0, ALU.mult))
            then(dve.tensor_tensor(KEEP1[:, :], keep, inverse, ALU.add))
            then(dve.tensor_tensor(inverse, prob, is0, ALU.mult))
            then(dve.tensor_tensor(SHARE[:, :], prob, inverse, ALU.subtract))
            counts, running, before = te(4), te(5), te(6)
            dve.wait_ge(ranks_done, 1)
            then(dve.tensor_copy(by_expert(counts), bank[7][:, 0:TE].rearrange("p (t e) -> p e t", e=EXPERTS)))
            then(dve.tensor_tensor_scan(running, const("keep"), counts, 0.0, ALU.mult, ALU.add))
            then(dve.tensor_tensor(before, running, counts, ALU.subtract))
            then(dve.tensor_tensor(by_expert(scratch), by_expert(running)[:, :, TILES - 1].unsqueeze(2).to_broadcast([P, EXPERTS, TILES]),
                                   const("thresholds").unsqueeze(1).to_broadcast([P, EXPERTS, TILES]), ALU.is_gt))
            then(dve.reduce_sum(per_e(0), by_expert(scratch), axis=AX.X))
            then(dve.tensor_tensor_scan(per_e(1), const("ones")[:, 0:EXPERTS], per_e(0), 0.0, ALU.mult, ALU.add))
            then(dve.tensor_tensor(per_e(2), per_e(1), per_e(0), ALU.subtract))
            then(dve.tensor_scalar(per_e(3), per_e(2), float(P), None, ALU.mult))
            then(dve.tensor_tensor(by_expert(before), by_expert(before), per_e(3).unsqueeze(2).to_broadcast([P, EXPERTS, TILES]), ALU.add))
            then(dve.tensor_tensor(by_tile(scratch), bank[0][:, 0:TE].rearrange("p (t e) -> p t e", e=EXPERTS),
                                   before.rearrange("p (e t) -> p t e", t=TILES), ALU.add))
            then(dve.tensor_tensor(scratch, scratch, onehot, ALU.mult))
            then(dve.reduce_sum(top, by_tile(scratch), axis=AX.X))
            dve.tensor_copy(SLOT[:, :], top).then_inc(slots_ready, 1)
            cmp = GCMP[0:1, :].rearrange("p (g e) -> p g e", e=EXPERTS)
            then(dve.tensor_tensor(cmp, per_e(1)[0:1, :].unsqueeze(1).to_broadcast([1, GROUPS, EXPERTS]),
                                   const("groups", 1).unsqueeze(2).to_broadcast([1, GROUPS, EXPERTS]), ALU.is_le))
            then(dve.reduce_sum(SMALL[0:1, 8 * TILES:8 * TILES + GROUPS], cmp, axis=AX.X))
            dve.tensor_scalar(GROUP_EXPERT[0:1, :], SMALL[0:1, 8 * TILES:8 * TILES + GROUPS], float(EXPERTS - 1), None,
                              ALU.min).then_inc(groups_ready, 1)
            dve.wait_ge(groups_ready, 1)

            for t in range(TILES):
                last = dve.scalar_tensor_tensor(out=H[:, t * D:t * D + D].rearrange("p (g n) -> p g n", g=2),
                                                in0=COMMON[:, :, t * (D // 2):(t + 1) * (D // 2)], scalar=KEEP1[:, t:t + 1],
                                                in1=H[:, t * D:t * D + D].rearrange("p (g n) -> p g n", g=2), op0=ALU.mult, op1=ALU.add)
            then(last)

            def group_step(i, ks):
                kh, = ks
                n, par, half = tile_at(i, kh)
                take_ht(TILES + n, True)
                expert = dve.value_load(GROUP_EXPERT[0:1, bass.ds(n, 1)], min_val=0, max_val=EXPERTS - 1)
                dve.wait_ge(y_done, TILES + n + 1)
                if kh >= 2:
                    dve.wait_ge(y_stored[par], 16 * half)
                dve.tensor_tensor(YR[par], bank[6][:, 0:D], B2[:, bass.ds(expert * D, D)], ALU.add).then_inc(y_used, 1)

            for n in range(2):
                group_step(0, [n])
            with dve.Fori(0, (GROUPS - 2) // 2) as i:
                for u in range(2):
                    group_step(i, [2 + u])

            for t in range(TILES):
                dve.wait_ge(gathered[t % 4], 16 * (t // 4 + 1))
                if t >= 4:
                    dve.wait_ge(out_stored[t % 4], 16 * (t // 4))
                dve.scalar_tensor_tensor(out=OUTR[t % 4], in0=GR[t % 4], scalar=SHARE[:, t:t + 1], in1=H[:, t * D:t * D + D],
                                         op0=ALU.mult, op1=ALU.add).then_inc(mixed, 1)

        @block.gpsimd
        def _(pool):
            pool.memset(NEGHALF[:, :], -0.5).then_inc(zeroed, 1)
            pool.memset(SB[0][:, 0:D], 0.0).then_inc(zeroed, 1)
            def add_bias(t0, t1):
                h = H[:, t0 * D:t1 * D].rearrange("p (t d) -> p t d", d=D)
                pool.tensor_tensor(h, h, CB[:, :].unsqueeze(1).to_broadcast([P, t1 - t0, D]), ALU.add).then_inc(h_set, 1)

            pool.wait_ge(pos_in[0], 32)
            add_bias(0, FIRST_ROWS)
            pool.wait_ge(zeroed, 2)
            pool.dma_start(packed.rearrange("(g p) d -> p g d", p=P),
                           SB[0][:, 0:D].unsqueeze(1).to_broadcast([P, GROUPS, D])).then_inc(packed_zeroed, 16)

            def patch_step(i, ks):
                kh, kq, kx = ks
                if kh == 1:
                    pool.wait_ge(pos_in[1], 16)
                    add_bias(FIRST_ROWS, TILES)
                if kh is not None:
                    t, par, half = tile_at(i, kh)
                    if kh >= 1:
                        pool.wait_ge(h_rstd, t)
                    pool.wait_ge(h_aggr, t + 1)
                    ride(pool)
                    pool.tensor_scalar(VE[:, 0:1], MVH[par][:, 1:2], EPS, None, ALU.add).then_inc(ve_h, 1)
                if kq is not None:
                    t, par, half = tile_at(i, kq)
                    if kq >= 1:
                        pool.wait_ge(qk_rstd, t)
                    pool.wait_ge(qk_aggr, t + 1)
                    ride(pool)
                    pool.tensor_scalar(VE[:, 1:3], MVQK[par].rearrange("p (j s) -> p j s", s=2)[:, :, 1], EPS, None, ALU.add).then_inc(ve_qk, 1)
                if kh is not None:
                    t, par, half = tile_at(i, kh)
                    pool.wait_ge(ve_h, t + 1)
                    pool.tensor_tensor(RSH[par][:, :], VE[:, 0:1], NEGHALF[:, 0:1], ALU.pow).then_inc(h_rstd, 1)
                if kq is not None:
                    t, par, half = tile_at(i, kq)
                    pool.wait_ge(ve_qk, t + 1)
                    pool.tensor_tensor(RSQK[par][:, :], VE[:, 1:3], NEGHALF[:, 0:2], ALU.pow).then_inc(qk_rstd, 1)
                if kx is not None:
                    t, par, half = tile_at(i, kx)
                    pool.wait_ge(xn_ready, t + 1)
                    h = H[:, bass.ds(t * D, D)]
                    pool.tensor_tensor(h, h, XN[par], ALU.add).then_inc(h_plus_xn, 1)

            two_by_two(pool, patch_step, (0, 2, 1), TILES)

            pool.wait_ge(gains_ready, 1)
            pool.wait_ge(qkT_copied, TILES + 1)
            pool.wait_ge(packed_zeroed, 16)

            def spread(a, par, guard):
                if guard:
                    pool.wait_ge(scores_done, a - 1)
                width = HEADS_A * SEQ
                for n in range(STEP_IMAGES):
                    pool.tensor_tensor(KR[par][:, n * width:(n + 1) * width].rearrange("p (h q) -> p h q", q=SEQ),
                                       KA[:, bass.ds(a * STEP_TOKENS + n * SEQ, SEQ)].unsqueeze(1).to_broadcast([P, HEADS_A, SEQ]),
                                       GM[:, 0:HEADS_A].unsqueeze(2).to_broadcast([P, HEADS_A, SEQ]), ALU.mult)
                base, hb = STEP_IMAGES * width, HEADS - HEADS_A
                for n in range(STEP_IMAGES):
                    last = pool.tensor_tensor(KR[par][0:DB, base + n * hb * SEQ:base + (n + 1) * hb * SEQ].rearrange("p (h q) -> p h q", q=SEQ),
                                              KB[0:DB, bass.ds(a * STEP_TOKENS + n * SEQ, SEQ)].unsqueeze(1).to_broadcast([DB, hb, SEQ]),
                                              GM[0:DB, HEADS_A:HEADS].unsqueeze(2).to_broadcast([DB, hb, SEQ]), ALU.mult)
                last.then_inc(kr_ready, 1)

            for a in range(2):
                spread(a, a, False)
            with pool.Fori(0, (STEPS - 2) // 2) as i:
                for u in range(2):
                    spread(2 * i + 2 + u, u, True)

            def mixer_step(i, ks):
                kh, kx = ks
                if kh is not None:
                    t, par, half = tile_at(i, kh)
                    if kh >= 1:
                        pool.wait_ge(h2_rstd, t)
                    pool.wait_ge(h2_aggr, t + 1)
                    ride(pool)
                    pool.tensor_scalar(VE[:, 0:1], MVH[par][:, 1:2], EPS, None, ALU.add).then_inc(ve_h, 1)
                    pool.wait_ge(ve_h, TILES + t + 1)
                    pool.tensor_tensor(RSH[par][:, :], VE[:, 0:1], NEGHALF[:, 0:1], ALU.pow).then_inc(h2_rstd, 1)
                if kx is not None:
                    t, par, half = tile_at(i, kx)
                    pool.wait_ge(xn2_ready, t + 1)
                    pool.tensor_copy(XN2[:, bass.ds(t * D, D)], XR[par]).then_inc(xn2_saved, 1)

            two_by_two(pool, mixer_step, (0, 1), TILES)

            pool.wait_ge(slots_ready, 1)
            pool.wait_ge(xn2_saved, TILES)
            for t in range(TILES):
                pool.indirect_dma_start(packed, bass.IndirectOffsetOnAxis(ap=SLOT[:, t:t + 1], axis=0),
                                        XN2[:, t * D:t * D + D], None).then_inc(scattered, 16)
            for par in range(2):
                pool.wait_ge(y_stored[par], 16 * GROUPS // 2)
            for t in range(TILES):
                if t >= 4:
                    pool.wait_ge(mixed, t - 3)
                pool.indirect_dma_start(GR[t % 4], None, packed_y,
                                        bass.IndirectOffsetOnAxis(ap=SLOT[:, t:t + 1], axis=0)).then_inc(gathered[t % 4], 16)


def _consts(np):
    c = np.zeros((P, NCONST), np.float32)

    def put(name, value):
        a, b = CONSTS[name]
        c[:, a:b] = value

    put("ident", np.eye(P))
    put("before", np.triu(np.ones((P, P)), 1))
    put("ones", 1.0)
    put("first", np.arange(EXPERTS, 0, -1))
    put("thresholds", np.arange(TILES) * P)
    put("groups", np.arange(GROUPS))
    put("keep", np.tile(np.arange(TILES) > 0, EXPERTS))
    row = np.arange(P)[:, None]
    put("heads_a", row // HD == np.arange(HEADS_A))
    put("heads_b", row // HD == np.arange(HEADS - HEADS_A))
    put("parity", row // SEQ == np.arange(2))
    return c


def _position_rows(np):
    edges = np.arange(1.0 / POS_TABLE_SIDE, 1.0, 1.0 / POS_TABLE_SIDE, dtype=np.float32)
    at = np.searchsorted(edges, np.arange(0.0, 1.0 - 1e-06, 1.0 / GRID, dtype=np.float32), side="right")
    return (at[:, None] * POS_TABLE_SIDE + at).reshape(-1)


def kernel(**inputs):
    import numpy as np
    import concourse.bacc as _bacc
    from concourse.bass_utils import run_bass_kernel_spmd as _run

    g = {k: np.asarray(v) for k, v in inputs.items()}

    def with_row(w, b):
        return np.concatenate([w, b[None]], axis=0)

    x = g["x"].reshape(IMAGES, CHANNELS, GRID, PATCH, GRID, PATCH).transpose(1, 3, 5, 0, 2, 4)
    x = x.reshape(KC, P, TILES, P).transpose(2, 1, 0, 3).reshape(TILES, P, KC * P)
    zero = np.zeros((D,), np.float32)
    w_qkv = np.concatenate([with_row(g["L0_attn_Wq"].T, zero), with_row(g["L0_attn_Wk"].T, g["L0_attn_bk"]),
                            with_row(g["L0_attn_Wv"].T, g["L0_attn_bv"])], axis=1)
    pos = g["L0_tok_pos_table"][_position_rows(np)]
    pos = np.tile(pos, (IMAGES, 1)).reshape(TILES, P, D).transpose(1, 0, 2).reshape(P, TILES * D)
    w1 = g["L0_ffn_W1"].transpose(1, 0, 2).reshape(D, EXPERTS * DFF)
    arrays = {
        "patches": x,
        "conv_w": g["L0_tok_conv_w"].reshape(D, KC, P).transpose(2, 1, 0).reshape(P, KC * D),
        "conv_b": np.tile(g["L0_tok_conv_b"], (P, 1)),
        "pos": pos,
        "w_qkv": w_qkv,
        "w_o": with_row(g["L0_attn_Wo"].T, g["L0_attn_bo"]),
        "gq": g["L0_attn_gq"][:, None],
        "gk": g["L0_attn_gk"][:, None],
        "w_router": with_row(g["L0_ffn_Ws"], g["L0_ffn_bs"]),
        "w1": w1[0:P],
        "w1_rest": with_row(w1[P:D], g["L0_ffn_b1"].reshape(-1)),
        "w2": g["L0_ffn_W2"].reshape(EXPERTS, FC, P, D).transpose(2, 0, 1, 3).reshape(P, EXPERTS * FC * D),
        "b2": np.tile(g["L0_ffn_b2"].reshape(1, -1), (P, 1)),
        "consts": _consts(np),
    }
    arrays = {f"in_{k}": np.ascontiguousarray(v) for k, v in arrays.items()}
    nc = _bacc.Bacc("TRN2", target_bir_lowering=False, num_devices=1)
    args = [nc.dram_tensor(k, v.shape, F32, kind="ExternalInput").ap() for k, v in arrays.items()]
    out = nc.dram_tensor("out", (TOKENS, D), F32, kind="ExternalOutput").ap()
    vit_kernel(nc, *args, out)
    r = _run(nc, [arrays], core_ids=[0])
    return r.results[0]["out"].reshape(IMAGES, SEQ, D)
```

```python
from contextlib import ExitStack

import concourse.bass as bass
from concourse import mybir

F32 = mybir.dt.float32
I32 = mybir.dt.int32
ALU = mybir.AluOpType
ACT = mybir.ActivationFunctionType
AX = mybir.AxisListType

P = 128
IMAGES, CHANNELS, SIDE = 64, 3, 96
PATCH = 16
GRID = SIDE // PATCH
SEQ = GRID * GRID
TOKENS = IMAGES * SEQ
TILES = TOKENS // P
D = 192
DB = D - P
PIXELS = CHANNELS * PATCH * PATCH
KC = PIXELS // P
HEADS, HD = 12, 16
HEADS_A = P // HD
PAIRS = HEADS // 2
DFF = 768
FC = DFF // P
FH = DFF // 2
EXPERTS = 9
EPS = 1e-5
GROUPS = (TOKENS + (EXPERTS - 1) * (P - 1)) // P
AHEAD = 8
XF_TILES = TILES - AHEAD + 1
ROW = D + 2
STEP_IMAGES = 2
ROW_PARTS = ((0, 2), (2, 8), (8, TILES))
STEPS = IMAGES // STEP_IMAGES
BASES_FIRST = 12
PAIR_STEPS = STEPS // 2
SPREAD_LAG, SCORE_LAG, WEIGH_LAG = 6, 7, 8
STEP_TOKENS = STEP_IMAGES * SEQ
K2 = 2 * SEQ
TE = TILES * EXPERTS
POS_TABLE_SIDE = 32

CONSTS = {}
_at = 0
for _name, _n in (("ident", P), ("before", P), ("ones", P), ("first", EXPERTS), ("thresholds", TILES),
                  ("groups", GROUPS), ("keep", TE), ("heads_a", HEADS_A), ("heads_b", HEADS - HEADS_A),
                  ("parity", 2)):
    CONSTS[_name] = (_at, _at + _n)
    _at += _n
NCONST = _at


def tile_at(i, k):
    return 2 * i + k, k % 2, i + k // 2


def vit_kernel(nc, patches, conv_w, conv_b, pos, w_qkv, w_o, gq, gk, w_router, w1, w1_rest, w2, b2, consts, ids, out):
    packed = nc.dram_tensor("packed_tokens", (GROUPS * P, ROW), F32, kind="Internal").ap()
    v_dram = nc.dram_tensor("v_rows", (TOKENS, D), F32, kind="Internal").ap()
    v_by_image = v_dram.rearrange("(n k) d -> k n d", k=SEQ)

    with ExitStack() as ctx:
        def sb(name, cols, dt=F32):
            return ctx.enter_context(nc.sbuf_tensor(name, [P, cols], dt))

        def sem(name):
            return ctx.enter_context(nc.semaphore(name))

        bank = [ctx.enter_context(nc.psum_tensor(f"bank{i}", [P, 512], F32)) for i in range(8)]

        W1A = sb("W1A", EXPERTS * DFF)
        W1B = sb("W1B", EXPERTS * DFF)
        W2 = sb("W2", EXPERTS * FC * D)
        B2 = sb("B2", EXPERTS * D)
        H = sb("H", TILES * D)
        QK = sb("QK", 4 * TOKENS)
        CST = sb("CST", NCONST)
        WO = sb("WO", 2 * D)
        WR = sb("WR", 2 * EXPERTS)
        NEGHALF = sb("NEGHALF", 2)
        LOG = sb("LOG", TE)
        KEEP1 = sb("KEEP1", TILES)
        SHARE = sb("SHARE", TILES)
        SLOT = sb("SLOT", TILES, I32)
        IDS = sb("IDS", TILES, I32)
        SLOT_ROWS = sb("SLOT_ROWS", 2 * GROUPS)
        ID = [sb(f"ID{i}", 1, I32) for i in range(2)]
        GROUP_EXPERT = sb("GROUP_EXPERT", GROUPS, I32)

        def const(name, rows=P):
            a, b = CONSTS[name]
            return CST[0:rows, a:b]

        ARENA = sb("ARENA", 5800)
        marks = [0]

        def cut(n):
            a = marks[0]
            marks[0] += n
            assert marks[0] <= 5800
            return ARENA[:, a:a + n]

        PT = [cut(KC * P) for _ in range(2)]
        CW = cut(KC * D)
        WQKV = [cut(3 * D) for _ in range(2)]
        XN = [cut(D) for _ in range(2)]
        QKN = [cut(2 * D) for _ in range(2)]
        VST = [cut(D) for _ in range(2)]
        marks[0] = 0
        HT = [cut(DFF) for _ in range(2)]
        XR = [cut(D) for _ in range(2)]
        XF = [cut(ROW) for _ in range(2)]
        YR = [cut(D) for _ in range(2)]
        OR = [cut(2 * P) for _ in range(2)]
        BASE = [cut(D) for _ in range(4)]
        RT = cut(8 * TE)

        RINGS = sb("RINGS", 3600)

        def ring(at, n):
            return [RINGS[:, at + i * n:at + (i + 1) * n] for i in range(2)]

        nk, ns = STEP_IMAGES * HEADS * SEQ, STEP_IMAGES * PAIRS * SEQ
        KR = ring(0, nk)
        SB = ring(2 * nk, ns)
        PR = ring(2 * (nk + ns), ns)
        W1R = ring(0, 2 * DFF)
        XTF = ring(4 * DFF, 2 * P)

        XT = [sb(f"XT{i}", 2 * P) for i in range(2)]
        V2 = [sb(f"V2{i}", STEP_IMAGES * D) for i in range(2)]
        VS = [sb(f"VS{i}", STEP_IMAGES * D) for i in range(2)]
        NP2 = STEP_IMAGES * PAIRS
        MX = sb("MX", NP2)
        SM = sb("SM", NP2)
        RC = sb("RC", NP2)
        R2 = sb("R2", 2 * NP2)
        GAIN = sb("GAIN", 4)
        GM = sb("GM", HEADS)
        STH = sb("STH", 6)
        STQK = sb("STQK", 12)
        MVH = [sb(f"MVH{i}", 2) for i in range(2)]
        MVQK = [sb(f"MVQK{i}", 4) for i in range(2)]
        RSH = [sb(f"RSH{i}", 1) for i in range(2)]
        RSQK = [sb(f"RSQK{i}", 2) for i in range(2)]
        VE = sb("VE", 3)
        CB = sb("CB", D)
        SMALL = sb("SMALL", 16 * TILES)
        SMALLE = sb("SMALLE", 8 * EXPERTS)
        GCMP = sb("GCMP", GROUPS * EXPERTS)

        QA, QB = QK[:, 0:TOKENS], QK[:, TOKENS:2 * TOKENS]
        KA, KB = QK[:, 2 * TOKENS:3 * TOKENS], QK[:, 3 * TOKENS:4 * TOKENS]
        XN2 = QK[:, 2 * TOKENS:2 * TOKENS + TILES * ROW]
        COMMON = QK[:, 0:2 * TOKENS].rearrange("p (g n) -> p g n", g=2)

        consts_in = sem("consts_in")
        pos_in = [sem(f"pos_in{i}") for i in range(3)]
        gains_in = sem("gains_in")
        conv_w_in = sem("conv_w_in")
        qkv_w_in = sem("qkv_w_in")
        mixer_w_in = sem("mixer_w_in")
        expert_w_in = sem("expert_w_in")
        patch_in = [sem(f"patch_in{i}") for i in range(2)]
        gains_ready = sem("gains_ready")
        set_up = sem("set_up")
        h_set = sem("h_set")
        conv_done = sem("conv_done")
        h_added = sem("h_added")
        h_stats = sem("h_stats")
        h_aggr = sem("h_aggr")
        h_rstd = sem("h_rstd")
        xn_ready = sem("xn_ready")
        h_plus_xn = sem("h_plus_xn")
        xt_transposed = sem("xt_transposed")
        xt_copied = sem("xt_copied")
        qk_done = sem("qk_done")
        v_done = sem("v_done")
        v_copied = sem("v_copied")
        v_stored = [sem(f"v_stored{i}") for i in range(2)]
        qk_stats = sem("qk_stats")
        qk_aggr = sem("qk_aggr")
        qk_rstd = sem("qk_rstd")
        qk_normed = sem("qk_normed")
        qkT_done = sem("qkT_done")
        qkT_copied = sem("qkT_copied")
        waited = sem("waited")
        ve_h = sem("ve_h")
        ve_qk = sem("ve_qk")
        kr_ready = sem("kr_ready")
        scores_done = sem("scores_done")
        max_ready = sem("max_ready")
        s_shifted = sem("s_shifted")
        exp_done = sem("exp_done")
        denom = sem("denom")
        v2_in = [sem(f"v2_in{i}") for i in range(2)]
        vs_ready = sem("vs_ready")
        pv_done = sem("pv_done")
        o_copied = sem("o_copied")
        or_ready = sem("or_ready")
        w_done = sem("w_done")
        h2_added = sem("h2_added")
        h2_stats = sem("h2_stats")
        h2_aggr = sem("h2_aggr")
        h2_rstd = sem("h2_rstd")
        xn2_ready = sem("xn2_ready")
        xn2_saved = sem("xn2_saved")
        ffn_t_done = sem("ffn_t_done")
        ffn_xt = sem("ffn_xt")
        f1_done = sem("f1_done")
        gelu_done = sem("gelu_done")
        xf_copied = sem("xf_copied")
        w1_copied = sem("w1_copied")
        xt1_done = sem("xt1_done")
        xt1_copied = sem("xt1_copied")
        y_done = sem("y_done")
        y_used = sem("y_used")
        router_done = sem("router_done")
        log_copied = sem("log_copied")
        rt = sem("rt")
        log_shifted = sem("log_shifted")
        log_exp = sem("log_exp")
        chosen = sem("chosen")
        ranks_done = sem("ranks_done")
        slots_ready = sem("slots_ready")
        groups_ready = sem("groups_ready")
        zeroed = sem("zeroed")
        packed_zeroed = sem("packed_zeroed")
        scattered = sem("scattered")
        xr_in = [sem(f"xr_in{i}") for i in range(2)]
        rows_tagged = sem("rows_tagged")
        slot_rows_in = sem("slot_rows_in")
        id_ready = sem("id_ready")
        y_biased = sem("y_biased")
        y_scaled = sem("y_scaled")
        y_added = [sem(f"y_added{i}") for i in range(2)]
        base_ready = sem("base_ready")
        out_stored = [sem(f"out_stored{i}") for i in range(4)]

        block = ctx.enter_context(nc.Block())

        def ride(e):
            e.sem_inc(waited, 1)

        def two_by_two(e, step, lags, tiles, after=None, counts=None, start=0):
            counts = counts or [tiles] * len(lags)
            last = max(lags)
            end = max(lag + count for lag, count in zip(lags, counts))
            first = last + 2 + (tiles - last) % 2
            assert first < tiles <= min(lag + count for lag, count in zip(lags, counts))

            def alone(s):
                step(0, [s - lag if 0 <= s - lag < count else None for lag, count in zip(lags, counts)])

            for s in range(start, first):
                alone(s)
            with e.Fori(0, (tiles - first) // 2) as i:
                for u in range(2):
                    step(i, [first + u - lag for lag in lags])
            for s in range(tiles, end):
                alone(s)
                if after:
                    after(s)

        @block.sync
        def _(sp):
            def h_rows(t0, t1):
                return slice(t0 * D, t1 * D)

            def load_rows(part):
                t0, t1 = ROW_PARTS[part]
                sp.dma_start(H[:, h_rows(t0, t1)], pos[:, h_rows(t0, t1)]).then_inc(pos_in[part], 16)

            sp.dma_start(PT[0], patches[0]).then_inc(patch_in[0], 16)
            sp.dma_start(CW, conv_w).then_inc(conv_w_in, 16)
            sp.dma_start(CB[:], conv_b).then_inc(pos_in[0], 16)
            load_rows(0)
            sp.dma_start(PT[1], patches[1]).then_inc(patch_in[1], 16)
            sp.dma_start(CST[:], consts).then_inc(consts_in, 16)
            sp.dma_start(WQKV[0], w_qkv[0:P]).then_inc(qkv_w_in, 16)
            sp.dma_start(WQKV[1][0:DB + 1], w_qkv[P:D + 1]).then_inc(qkv_w_in, 16)
            load_rows(1)

            def load_patch(t, par):
                sp.wait_ge(conv_done, t - 1)
                sp.dma_start(PT[par], patches[bass.ds(t, 1)].rearrange("a p n -> (a p) n")).then_inc(patch_in[par], 16)

            def store_v(t, par):
                sp.wait_ge(v_copied, t + 1)
                sp.dma_start(v_dram[bass.ds(t * P, P)], VST[par]).then_inc(v_stored[par], 16)

            def load_up(e):
                cols = bass.ds(e * DFF, DFF)
                sp.dma_start(W1A[:, cols], w1[:, cols]).then_inc(expert_w_in, 16)
                sp.dma_start(W1B[0:DB + 1, cols], w1_rest[:, cols]).then_inc(expert_w_in, 16)

            def load_down(e):
                cols = bass.ds(e * FC * D, FC * D)
                sp.dma_start(W2[:, cols], w2[:, cols]).then_inc(expert_w_in, 16)

            def v2_load(p, i, k):
                sp.wait_ge(v_stored[0], 16 * (i + (k + 2) // 2 + 1))
                sp.wait_ge(v_stored[1], 16 * (i + (k + 1) // 2 + 1))
                for par in range(2):
                    a = 2 * p + par
                    if k >= 1:
                        sp.wait_ge(vs_ready, a - 1)
                    for copy in range(2):
                        sp.dma_start(V2[par][copy * SEQ:copy * SEQ + SEQ, :].rearrange("p (n d) -> p n d", n=STEP_IMAGES),
                                     v_by_image[:, bass.ds(a * STEP_IMAGES, STEP_IMAGES), :]).then_inc(v2_in[par], 16)

            def load_step(i, ks):
                kp, kv, k2, ke = ks
                if kp == 4:
                    load_rows(2)
                    for row, g in enumerate((gq, gk)):
                        sp.dma_start(GAIN[:, row:row + 1], g[0:P]).then_inc(gains_in, 16)
                        sp.dma_start(GAIN[0:DB, 2 + row:3 + row], g[P:D]).then_inc(gains_in, 16)
                if kp is not None and kp >= 2:
                    t, par, half = tile_at(i, kp)
                    load_patch(t, par)
                if kv is not None:
                    t, par, half = tile_at(i, kv)
                    store_v(t, par)
                if k2 is not None:
                    v2_load(tile_at(i, k2)[0], i, k2)
                if ke is not None:
                    load_up(tile_at(i, ke)[0])
                    load_down(tile_at(i, ke)[0])

            two_by_two(sp, load_step, (0, 4, SPREAD_LAG + 2, TILES - EXPERTS), TILES,
                       counts=(TILES, TILES, PAIR_STEPS, EXPERTS))
            sp.dma_start(B2[:], b2).then_inc(expert_w_in, 16)
            for dst, src in ((WO[:, 0:D], w_o[0:P]), (WO[0:DB + 1, D:2 * D], w_o[P:D + 1]),
                             (WR[:, 0:EXPERTS], w_router[0:P]), (WR[0:DB + 1, EXPERTS:2 * EXPERTS], w_router[P:D + 1])):
                sp.dma_start(dst, src).then_inc(mixer_w_in, 16)
            sp.dma_start(IDS[:], ids).then_inc(mixer_w_in, 16)

            def store_base(t):
                sp.wait_ge(base_ready, t + 1)
                sp.dma_start(out[t * P:t * P + P], BASE[t % 4]).then_inc(out_stored[t % 4], 16)

            for t in range(BASES_FIRST):
                store_base(t)
            sp.wait_ge(scattered, 16 * TILES)
            sp.wait_ge(ffn_t_done, XF_TILES)
            for r in range(2):
                sp.dma_start(XF[r], packed[r * P:r * P + P]).then_inc(xr_in[r], 16)
            sp.dma_start(SLOT_ROWS[:, :].rearrange("p (g w) -> p g w", w=2),
                         packed.rearrange("(g p) w -> p g w", p=P)[:, :, D:ROW]).then_inc(slot_rows_in, 16)
            for t in range(BASES_FIRST, TILES):
                store_base(t)

            def load_group(i, ks):
                n, par, half = tile_at(i, ks[0])
                sp.wait_ge(ffn_t_done, TILES + n - 1)
                sp.dma_start(XF[par], packed[bass.ds(n * P, P)]).then_inc(xr_in[par], 16)

            two_by_two(sp, load_group, (0,), GROUPS, start=2)
            for ring4 in range(4):
                sp.wait_ge(out_stored[ring4], 16 * len(range(ring4, TILES, 4)))
            for par in range(2):
                sp.wait_ge(y_added[par], 16 * len(range(par, GROUPS, 2)))

        @block.tensor
        def _(pe):
            ident = const("ident")

            def conv(i, k):
                t, par, half = tile_at(i, k)
                pe.wait_ge(patch_in[par], 16 * (half + 1))
                if k >= 1:
                    pe.wait_ge(h_added, t)
                for c in range(KC):
                    last = pe.matmul(bank[0][:, 0:D], PT[par][:, c * P:c * P + P], CW[:, c * D:c * D + D],
                                     start=c == 0, stop=c == KC - 1)
                last.then_inc(conv_done, 1)

            def transpose_tile(src, dst):
                pe.transpose(dst[:, 0:P], src[:, 0:P], ident)
                return pe.transpose(dst[0:DB, P:2 * P], src[:, P:D], ident)

            def transpose_xn(i, k):
                t, par, half = tile_at(i, k)
                pe.wait_ge(xn_ready, t + 1)
                if k == 0:
                    pe.wait_ge(consts_in, 16)
                if k >= 3:
                    pe.wait_ge(qkT_copied, t - 2)
                transpose_tile(XN[par], bank[1]).then_inc(xt_transposed, 1)

            def project(i, k):
                t, par, half = tile_at(i, k)
                pe.wait_ge(xt_copied, t + 1)
                if k == 0:
                    pe.wait_ge(qkv_w_in, 32)
                    pe.wait_ge(set_up, 2)
                if k >= 1:
                    pe.wait_ge(qk_normed, t)
                x = XT[par]
                pe.matmul(bank[2][:, 0:2 * D], x[:, 0:P], WQKV[0][:, 0:2 * D], start=True, stop=False)
                pe.matmul(bank[2][:, 0:2 * D], x[0:DB + 1, P:2 * P], WQKV[1][0:DB + 1, 0:2 * D], start=False, stop=True).then_inc(qk_done, 1)
                if k >= 1:
                    pe.wait_ge(v_copied, t)
                pe.matmul(bank[3][:, 0:D], x[:, 0:P], WQKV[0][:, 2 * D:3 * D], start=True, stop=False)
                pe.matmul(bank[3][:, 0:D], x[0:DB + 1, P:2 * P], WQKV[1][0:DB + 1, 2 * D:3 * D], start=False, stop=True).then_inc(v_done, 1)

            def transpose_qk(i, k):
                t, par, half = tile_at(i, k)
                pe.wait_ge(qk_normed, t + 1)
                pe.wait_ge(xt_copied, min(t + 3, TILES) if isinstance(t, int) else t + 3)
                n = QKN[par]
                for j in range(2):
                    pe.transpose(bank[1][:, j * P:j * P + P], n[:, j * D:j * D + P], ident)
                for j in range(2):
                    last = pe.transpose(bank[1][0:DB, (2 + j) * P:(3 + j) * P], n[:, j * D + P:j * D + D], ident)
                last.then_inc(qkT_done, 1)

            def scores(p, par, k):
                a = 2 * p + par
                pe.wait_ge(kr_ready, a + 1)
                if k >= 1:
                    pe.wait_ge(s_shifted, a - 1)
                ka = KR[par][:, 0:STEP_IMAGES * HEADS_A * SEQ]
                kb = KR[par][0:DB, STEP_IMAGES * HEADS_A * SEQ:]
                for n in range(STEP_IMAGES):
                    for j in range(PAIRS):
                        if j < HEADS_A // 2:
                            at = n * HEADS_A * SEQ + j * K2
                            keys, queries = ka[:, at:at + K2], QA[:, bass.ds(a * STEP_TOKENS + n * SEQ, SEQ)]
                        else:
                            at = n * (HEADS - HEADS_A) * SEQ + (j - HEADS_A // 2) * K2
                            keys, queries = kb[:, at:at + K2], QB[0:DB, bass.ds(a * STEP_TOKENS + n * SEQ, SEQ)]
                        o = (n * PAIRS + j) * SEQ
                        last = pe.matmul(bank[4 + par][0:K2, o:o + SEQ], keys, queries, start=True, stop=True)
                last.then_inc(scores_done, 1)

            def weigh_v(p, par):
                a = 2 * p + par
                pe.wait_ge(vs_ready, a + 1)
                pe.wait_ge(o_copied, a + 1)
                for n in range(STEP_IMAGES):
                    for j in range(PAIRS):
                        at = n * PAIRS + j
                        row = 32 * (j % 4)
                        col = (j // 4) * STEP_TOKENS + n * SEQ
                        last = pe.matmul(bank[6 + par][row:row + 32, col:col + SEQ], VS[par][0:K2, at * 32:at * 32 + 32],
                                         PR[par][0:K2, at * SEQ:at * SEQ + SEQ], start=True, stop=True)
                last.then_inc(pv_done, 1)

            def patch_step(i, ks):
                kc, kq, kp, kx, k_scores, k_weigh = ks
                if kc is not None:
                    conv(i, kc)
                if k_scores is not None:
                    scores(tile_at(i, k_scores)[0], 0, k_scores)
                if k_weigh is not None:
                    weigh_v(tile_at(i, k_weigh)[0], 0)
                if kq is not None:
                    transpose_qk(i, kq)
                if k_scores is not None:
                    scores(tile_at(i, k_scores)[0], 1, k_scores)
                if kp is not None:
                    project(i, kp)
                if k_weigh is not None:
                    weigh_v(tile_at(i, k_weigh)[0], 1)
                if kx is not None:
                    transpose_xn(i, kx)

            pe.sem_inc(qkT_done, 2)
            pe.wait_ge(conv_w_in, 16)
            two_by_two(pe, patch_step, (0, 4, 2, 1, SCORE_LAG, WEIGH_LAG), TILES,
                       counts=(TILES,) * 4 + (PAIR_STEPS,) * 2)

            def project_o(i, k):
                t, par, half = tile_at(i, k)
                pe.wait_ge(or_ready, t + 1)
                if k >= 1:
                    pe.wait_ge(h2_added, t)
                o = OR[par]
                pe.matmul(bank[0][:, 0:D], o[:, 0:P], WO[:, 0:D], start=True, stop=False)
                pe.matmul(bank[0][:, 0:D], o[0:DB + 1, P:2 * P], WO[0:DB + 1, D:2 * D], start=False, stop=True).then_inc(w_done, 1)

            def ffn_transpose(n, rows, guard):
                if guard:
                    pe.wait_ge(ffn_xt, n)
                transpose_tile(rows, bank[4]).then_inc(ffn_t_done, 1)

            def ffn_up(n, par, first, rest, guard):
                pe.wait_ge(ffn_xt, n + 1)
                x = XTF[par]
                for c in range(FC):
                    g, at = c // (FC // 2), c % (FC // 2) * P
                    if guard and at == 0:
                        pe.wait_ge(gelu_done, 2 * n - 1 + g)
                    pe.matmul(bank[2 + g][:, at:at + P], first[:, c * P:c * P + P], x[:, 0:P], start=True, stop=False)
                    last = pe.matmul(bank[2 + g][:, at:at + P], rest[0:DB + 1, c * P:c * P + P], x[0:DB + 1, P:2 * P],
                                     start=False, stop=True)
                    if c % (FC // 2) == FC // 2 - 1:
                        last.then_inc(f1_done, 1)

            def ffn_down(n, par, expert, guard):
                if guard:
                    pe.wait_ge(y_used, n - 1)
                for c in range(FC):
                    if c % (FC // 2) == 0:
                        pe.wait_ge(gelu_done, 2 * n + 1 + c // (FC // 2))
                    last = pe.matmul(bank[5 + par][:, 0:D], HT[par][:, c * P:c * P + P], W2[:, bass.ds((expert * FC + c) * D, D)],
                                     start=c == 0, stop=c == FC - 1)
                last.then_inc(y_done, 1)

            def route(t, par, guard):
                if guard:
                    pe.wait_ge(log_copied, t)
                x = XT[par]
                pe.matmul(bank[7][:, 0:EXPERTS], x[:, 0:P], WR[:, 0:EXPERTS], start=True, stop=False)
                pe.matmul(bank[7][:, 0:EXPERTS], x[0:DB + 1, P:2 * P], WR[0:DB + 1, EXPERTS:2 * EXPERTS],
                          start=False, stop=True).then_inc(router_done, 1)

            def mixer_step(i, ks):
                kw, k1, kr, kt, kf, kh = ks
                if kf is not None:
                    t, par, half = tile_at(i, kf)
                    ffn_up(t, par, W1A, W1B, kf >= 1)
                if kt is not None:
                    t, par, half = tile_at(i, kt)
                    if kt < XF_TILES:
                        pe.wait_ge(xf_copied, t + 1)
                        ffn_transpose(t, XF[par], kt >= 1)
                    else:
                        ffn_transpose(t, XN2[:, t * ROW:t * ROW + D], True)
                if kw is not None:
                    project_o(i, kw)
                if kr is not None:
                    t, par, half = tile_at(i, kr)
                    pe.wait_ge(xt1_copied, t + 1)
                    route(t, par, kr >= 1)
                if kh is not None:
                    t, par, half = tile_at(i, kh)
                    ffn_down(t, par, 0, kh >= 2)
                if k1 is not None:
                    t, par, half = tile_at(i, k1)
                    pe.wait_ge(xn2_ready, t + 1)
                    if k1 >= 1:
                        pe.wait_ge(xt1_copied, t)
                    transpose_tile(XR[par], bank[1]).then_inc(xt1_done, 1)

            def count_ranks(s):
                if s == TILES + 1:
                    pe.wait_ge(chosen, 1)
                    onehot = RT[:, 0:TE]
                    pe.wait_ge(h2_added, TILES)
                    pe.matmul(bank[0][:, 0:TE], const("before"), onehot, start=True, stop=True)
                    pe.matmul(bank[7][:, 0:TE], const("ones"), onehot, start=True, stop=True).then_inc(ranks_done, 1)

            pe.wait_ge(o_copied, STEPS + 2)
            pe.wait_ge(mixer_w_in, 16 * 5)
            pe.wait_ge(expert_w_in, 16 * (3 * EXPERTS + 1))
            pe.wait_ge(set_up, 6)
            two_by_two(pe, mixer_step, (0, 1, 2, AHEAD, AHEAD + 1, AHEAD + 2), TILES, count_ranks)

            def group_step(i, ks):
                kt, kf, kh = ks
                if kf is not None:
                    n, par, half = tile_at(i, kf)
                    pe.wait_ge(w1_copied, n + 1)
                    ffn_up(TILES + n, par, W1R[par][:, 0:DFF], W1R[par][:, DFF:2 * DFF], True)
                if kt is not None:
                    n, par, half = tile_at(i, kt)
                    pe.wait_ge(xr_in[par], 16 * (half + 1))
                    ffn_transpose(TILES + n, XF[par], True)
                if kh is not None:
                    n, par, half = tile_at(i, kh)
                    expert = pe.value_load(GROUP_EXPERT[0:1, bass.ds(n, 1)], min_val=0, max_val=EXPERTS - 1)
                    ffn_down(TILES + n, par, expert, True)

            pe.wait_ge(groups_ready, 1)
            two_by_two(pe, group_step, (0, 1, 2), GROUPS)

        @block.scalar
        def _(act):
            def copy_xt(dst, src):
                act.activation(dst[:, 0:P], src[:, 0:P], ACT.Copy)
                return act.activation(dst[0:DB, P:2 * P], src[0:DB, P:2 * P], ACT.Copy)

            def exp_scores(p, par, k):
                a = 2 * p + par
                act.wait_ge(s_shifted, a + 1)
                if k >= 1:
                    act.wait_ge(pv_done, a - 1)
                act.activation(PR[par][0:K2, :], SB[par][0:K2, :], ACT.Exp, scale=HD ** -0.5).then_inc(exp_done, 1)

            def copy_o(p, par):
                a = 2 * p + par
                act.wait_ge(pv_done, a + 1)
                act.activation(QA[:, bass.ds(a * STEP_TOKENS, STEP_TOKENS)], bank[6 + par][:, 0:STEP_TOKENS], ACT.Copy)
                act.activation(QB[0:DB, bass.ds(a * STEP_TOKENS, STEP_TOKENS)],
                               bank[6 + par][0:DB, STEP_TOKENS:2 * STEP_TOKENS], ACT.Copy).then_inc(o_copied, 1)

            def patch_step(i, ks):
                kx, kv, kq, k_exp, k_o = ks
                if k_exp is not None:
                    exp_scores(tile_at(i, k_exp)[0], 0, k_exp)
                if k_o is not None:
                    copy_o(tile_at(i, k_o)[0], 0)
                if kq is not None:
                    t, par, half = tile_at(i, kq)
                    act.wait_ge(qkT_done, t + 3)
                    qk = QK[:, :].rearrange("p (j g n) -> p j g n", j=2, g=2)
                    act.activation(qk[:, :, 0, bass.ds(t * P, P)],
                                   bank[1][:, 0:2 * P].rearrange("p (j n) -> p j n", j=2), ACT.Copy)
                    act.activation(qk[0:DB, :, 1, bass.ds(t * P, P)],
                                   bank[1][0:DB, 2 * P:4 * P].rearrange("p (j n) -> p j n", j=2), ACT.Copy).then_inc(qkT_copied, 1)
                if k_exp is not None:
                    exp_scores(tile_at(i, k_exp)[0], 1, k_exp)
                if kv is not None:
                    t, par, half = tile_at(i, kv)
                    act.wait_ge(v_done, t + 1)
                    if kv >= 2:
                        act.wait_ge(v_stored[par], 16 * half)
                    act.activation(VST[par], bank[3][:, 0:D], ACT.Copy).then_inc(v_copied, 1)
                if k_o is not None:
                    copy_o(tile_at(i, k_o)[0], 1)
                if kx is not None:
                    t, par, half = tile_at(i, kx)
                    act.wait_ge(xt_transposed, t + 1)
                    if kx >= 2:
                        act.wait_ge(v_done, t - 1)
                    copy_xt(XT[par], bank[1]).then_inc(xt_copied, 1)

            act.sem_inc(o_copied, 2)
            two_by_two(act, patch_step, (1, 2, 4, SCORE_LAG, WEIGH_LAG), TILES,
                       counts=(TILES,) * 3 + (PAIR_STEPS,) * 2)

            def gelu(n, par, guard):
                for g in range(2):
                    act.wait_ge(f1_done, 2 * n + 1 + g)
                    if guard and g == 0:
                        act.wait_ge(y_done, n - 1)
                    act.activation(HT[par][:, g * FH:g * FH + FH], bank[2 + g][:, 0:FH], ACT.Gelu).then_inc(gelu_done, 1)

            def copy_xf(n, par, guard):
                act.wait_ge(ffn_t_done, n + 1)
                if guard:
                    act.wait_ge(f1_done, 2 * (n - 1))
                copy_xt(XTF[par], bank[4]).then_inc(ffn_xt, 1)

            def mixer_step(i, ks):
                ko, kx, kt, kg = ks
                if kg is not None:
                    t, par, half = tile_at(i, kg)
                    gelu(t, par, kg >= 2)
                if kt is not None:
                    t, par, half = tile_at(i, kt)
                    copy_xf(t, par, kt >= 2)
                if ko is not None:
                    t, par, half = tile_at(i, ko)
                    if ko >= 2:
                        act.wait_ge(w_done, t - 1)
                    act.activation(OR[par][:, 0:P], QA[:, bass.ds(t * P, P)], ACT.Copy)
                    act.activation(OR[par][0:DB, P:2 * P], QB[0:DB, bass.ds(t * P, P)], ACT.Copy).then_inc(or_ready, 1)
                if kx is not None:
                    t, par, half = tile_at(i, kx)
                    act.wait_ge(xt1_done, t + 1)
                    if kx >= 2:
                        act.wait_ge(router_done, t - 1)
                    copy_xt(XT[par], bank[1]).then_inc(xt1_copied, 1)

            def exp_logits(s):
                if s == TILES + 2:
                    act.wait_ge(log_shifted, 1)
                    act.activation(RT[:, 3 * TE:4 * TE], RT[:, 2 * TE:3 * TE], ACT.Exp).then_inc(log_exp, 1)

            act.wait_ge(o_copied, STEPS + 2)
            act.wait_ge(set_up, 6)
            two_by_two(act, mixer_step, (0, 2, AHEAD + 1, AHEAD + 2), TILES, exp_logits)

            def group_step(i, ks):
                kx, kg = ks
                if kg is not None:
                    n, par, half = tile_at(i, kg)
                    gelu(TILES + n, par, True)
                if kx is not None:
                    n, par, half = tile_at(i, kx)
                    copy_xf(TILES + n, par, True)

            two_by_two(act, group_step, (0, 1), GROUPS)

        @block.vector
        def _(dve):
            def norm(dst, src, mv, rstd):
                return dve.tensor_scalar(dst, src, mv[:, 0:1], rstd, ALU.subtract, ALU.mult)

            for par in range(2):
                dve.memset(XT[par][DB:DB + 1, P:2 * P], 1.0).then_inc(set_up, 1)
            dve.wait_ge(h_set, 1)

            def attention_step(i, m, k_max, d, k_share):
                if k_share is not None:
                    p = tile_at(i, k_share)[0]
                    a = 2 * p + d
                    dve.wait_ge(exp_done, a + 1)
                    dve.reduce_sum(SM[0:K2, :], PR[d][0:K2, :].rearrange("p (m q) -> p m q", q=SEQ), axis=AX.X).then_inc(denom, 1)
                if k_max is not None:
                    b = 2 * tile_at(i, k_max)[0] + m
                    dve.wait_ge(scores_done, b + 1)
                    dve.reduce_max(MX[0:K2, :], bank[4 + m][0:K2, 0:NP2 * SEQ].rearrange("p (m q) -> p m q", q=SEQ), axis=AX.X).then_inc(max_ready, 1)
                if k_share is not None:
                    dve.wait_ge(denom, 3 * a + 1)
                    dve.reciprocal(RC[0:K2, :], SM[0:K2, :]).then_inc(denom, 1)
                if k_max is not None:
                    dve.wait_ge(max_ready, b + 1)
                    dve.tensor_tensor(SB[m][0:K2, :].rearrange("p (m q) -> p m q", q=SEQ),
                                      bank[4 + m][0:K2, 0:NP2 * SEQ].rearrange("p (m q) -> p m q", q=SEQ),
                                      MX[0:K2, :].unsqueeze(2).to_broadcast([K2, NP2, SEQ]), ALU.subtract).then_inc(s_shifted, 1)
                if k_share is not None:
                    dve.wait_ge(denom, 3 * a + 2)
                    dve.tensor_tensor(R2[0:K2, :].rearrange("p (m h) -> p m h", h=2),
                                      RC[0:K2, :].unsqueeze(2).to_broadcast([K2, NP2, 2]),
                                      const("parity", K2).unsqueeze(1).to_broadcast([K2, NP2, 2]), ALU.mult).then_inc(denom, 1)
                    dve.wait_ge(denom, 3 * a + 3)
                    dve.wait_ge(v2_in[d], 32 * (p + 1))
                    dve.tensor_tensor(VS[d][0:K2, :].rearrange("p (m d) -> p m d", d=HD),
                                      V2[d][0:K2, :].rearrange("p (m d) -> p m d", d=HD),
                                      R2[0:K2, :].unsqueeze(2).to_broadcast([K2, 2 * NP2, HD]), ALU.mult).then_inc(vs_ready, 1)

            def patch_step(i, ks):
                kh, kn, ks_, kq, k_max, k_share = ks
                if kn is not None:
                    t, par, half = tile_at(i, kn)
                    dve.wait_ge(h_rstd, t + 1)
                    if kn >= 2:
                        dve.wait_ge(xt_transposed, t - 1)
                        dve.wait_ge(h_plus_xn, t - 1)
                    norm(XN[par], H[:, bass.ds(t * D, D)], MVH[par], RSH[par][:, 0:1]).then_inc(xn_ready, 1)
                if kq is not None:
                    t, par, half = tile_at(i, kq)
                    dve.wait_ge(qk_rstd, t + 1)
                    dve.wait_ge(qkT_done, t + 1)
                    norm(QKN[par][:, 0:D], bank[2][:, 0:D], MVQK[par][:, 0:2], RSQK[par][:, 0:1])
                    norm(QKN[par][:, D:2 * D], bank[2][:, D:2 * D], MVQK[par][:, 2:4], RSQK[par][:, 1:2]).then_inc(qk_normed, 1)
                if kh == 4:
                    dve.wait_ge(consts_in, 16)
                    dve.wait_ge(gains_in, 64)
                    dve.tensor_scalar(GM[:, 0:HEADS_A], const("heads_a"), GAIN[:, 0:1], GAIN[:, 1:2], ALU.mult, ALU.mult)
                    dve.tensor_scalar(GM[0:DB, HEADS_A:HEADS], const("heads_b", DB), GAIN[0:DB, 2:3], GAIN[0:DB, 3:4],
                                      ALU.mult, ALU.mult).then_inc(gains_ready, 1)
                attention_step(i, 0, k_max, 1, k_share)
                if kh is not None:
                    t, par, half = tile_at(i, kh)
                    if kh in (2, 4, 6, 8):
                        dve.wait_ge(h_set, t // 2 + 1)
                    elif kh == 10:
                        dve.wait_ge(h_set, TILES // 2)
                    dve.wait_ge(conv_done, t + 1)
                    h = H[:, bass.ds(t * D, D)]
                    dve.tensor_tensor(h, bank[0][:, 0:D], h, ALU.add).then_inc(h_added, 1)
                    dve.wait_ge(h_added, t + 1)
                    ride(dve)
                    dve.bn_stats(STH[:, :], H[:, bass.ds(t * D, D)]).then_inc(h_stats, 1)
                    dve.wait_ge(h_stats, t + 1)
                    ride(dve)
                    dve.bn_aggr(MVH[par][:, :], STH[:, :]).then_inc(h_aggr, 1)
                attention_step(i, 1, k_max, 0, k_max)
                if ks_ is not None:
                    t, par, half = tile_at(i, ks_)
                    dve.wait_ge(qk_done, t + 1)
                    for j in range(2):
                        last = dve.bn_stats(STQK[:, 6 * j:6 * j + 6], bank[2][:, j * D:j * D + D])
                    last.then_inc(qk_stats, 1)
                    dve.wait_ge(qk_stats, t + 1)
                    ride(dve)
                    for j in range(2):
                        last = dve.bn_aggr(MVQK[par][:, 2 * j:2 * j + 2], STQK[:, 6 * j:6 * j + 6])
                    last.then_inc(qk_aggr, 1)

            two_by_two(dve, patch_step, (0, 1, 2, 3, SCORE_LAG, WEIGH_LAG), TILES,
                       counts=(TILES,) * 4 + (PAIR_STEPS,) * 2)

            def mixer_step(i, ks):
                kw, kl, kh = ks
                if kw is not None:
                    t, par, half = tile_at(i, kw)
                    dve.wait_ge(w_done, t + 1)
                    h = H[:, bass.ds(t * D, D)]
                    dve.tensor_tensor(h, bank[0][:, 0:D], h, ALU.add).then_inc(h2_added, 1)
                    dve.wait_ge(h2_added, t + 1)
                    ride(dve)
                    dve.bn_stats(STH[:, :], h).then_inc(h2_stats, 1)
                    dve.wait_ge(h2_stats, t + 1)
                    ride(dve)
                    dve.bn_aggr(MVH[par][:, :], STH[:, :]).then_inc(h2_aggr, 1)
                if kl is not None:
                    t, par, half = tile_at(i, kl)
                    dve.wait_ge(router_done, t + 1)
                    dve.tensor_copy(LOG[:, bass.ds(t * EXPERTS, EXPERTS)], bank[7][:, 0:EXPERTS]).then_inc(log_copied, 1)
                if kw is not None:
                    t, par, half = tile_at(i, kw)
                    dve.wait_ge(h2_rstd, t + 1)
                    if kw >= 2:
                        dve.wait_ge(xt1_done, t - 1)
                        dve.wait_ge(xn2_saved, t - 1)
                    norm(XR[par], H[:, bass.ds(t * D, D)], MVH[par], RSH[par][:, 0:1]).then_inc(xn2_ready, 1)
                if kl == TILES - 1:
                    choose()
                if kh == TILES - AHEAD:
                    slots()
                    shares()
                    group_experts()
                if kh is not None:
                    t, par, half = tile_at(i, kh)
                    dve.wait_ge(y_done, t + 1)
                    dve.tensor_tensor(COMMON[:, :, bass.ds(t * (D // 2), D // 2)],
                                      bank[5 + par][:, 0:D].rearrange("p (g n) -> p g n", g=2),
                                      B2[:, 0:D].rearrange("p (g n) -> p g n", g=2), ALU.add).then_inc(y_used, 1)

            steps = [0]

            def then(ins):
                steps[0] += 1
                ins.then_inc(rt, 1)
                dve.wait_ge(rt, steps[0])

            def te(n):
                return RT[:, n * TE:n * TE + TE]

            def by_tile(ap):
                return ap.rearrange("p (t e) -> p t e", e=EXPERTS)

            def by_expert(ap):
                return ap.rearrange("p (e t) -> p e t", t=TILES)

            def over_e(ap):
                return ap.unsqueeze(2).to_broadcast([P, TILES, EXPERTS])

            def over_t(ap):
                return ap.unsqueeze(1).to_broadcast([P, TILES, EXPERTS])

            def small(n):
                return SMALL[:, n * TILES:n * TILES + TILES]

            def per_e(n):
                return SMALLE[:, n * EXPERTS:n * EXPERTS + EXPERTS]

            onehot, scratch, shifted, exped = te(0), te(1), te(2), te(3)
            top, total, prob, inverse, is0, keep, pick = (small(n) for n in range(7))
            counts, running, before = te(4), te(5), te(6)

            def choose():
                dve.wait_ge(log_copied, TILES)
                then(dve.reduce_max(top, by_tile(LOG[:, :]), axis=AX.X))
                dve.tensor_tensor(by_tile(shifted), by_tile(LOG[:, :]), over_e(top), ALU.subtract).then_inc(log_shifted, 1)
                then(dve.tensor_tensor(by_tile(scratch), by_tile(LOG[:, :]), over_e(top), ALU.is_equal))
                then(dve.tensor_tensor(by_tile(scratch), by_tile(scratch), over_t(const("first")), ALU.mult))
                then(dve.reduce_max(pick, by_tile(scratch), axis=AX.X))
                dve.tensor_tensor(by_tile(onehot), over_t(const("first")), over_e(pick), ALU.is_equal).then_inc(chosen, 1)

            def shares():
                dve.wait_ge(log_exp, 1)
                then(dve.reduce_sum(total, by_tile(exped), axis=AX.X))
                then(dve.reciprocal(prob, total))
                then(dve.reciprocal(inverse, prob))
                dve.tensor_copy(is0, by_tile(onehot)[:, :, 0])
                then(dve.tensor_tensor(inverse, prob, inverse, ALU.mult))
                then(dve.tensor_scalar(keep, prob, -1.0, 1.0, ALU.mult, ALU.add))
                then(dve.tensor_tensor(inverse, inverse, keep, ALU.subtract))
                then(dve.tensor_tensor(inverse, inverse, is0, ALU.mult))
                then(dve.tensor_tensor(KEEP1[:, :], keep, inverse, ALU.add))
                then(dve.tensor_tensor(inverse, prob, is0, ALU.mult))
                then(dve.tensor_tensor(SHARE[:, :], prob, inverse, ALU.subtract))
                dve.wait_ge(xn2_saved, TILES)
                rows = XN2.rearrange("p (t w) -> p t w", w=ROW)
                dve.tensor_copy(rows[:, :, D], SHARE[:, :])
                dve.tensor_copy(rows[:, :, D + 1].bitcast(I32), IDS[:, :]).then_inc(rows_tagged, 1)

            def slots():
                dve.wait_ge(ranks_done, 1)
                then(dve.tensor_copy(by_expert(counts), bank[7][:, 0:TE].rearrange("p (t e) -> p e t", e=EXPERTS)))
                then(dve.tensor_tensor_scan(running, const("keep"), counts, 0.0, ALU.mult, ALU.add))
                then(dve.tensor_tensor(before, running, counts, ALU.subtract))
                then(dve.tensor_tensor(by_expert(scratch), by_expert(running)[:, :, TILES - 1].unsqueeze(2).to_broadcast([P, EXPERTS, TILES]),
                                       const("thresholds").unsqueeze(1).to_broadcast([P, EXPERTS, TILES]), ALU.is_gt))
                then(dve.reduce_sum(per_e(0), by_expert(scratch), axis=AX.X))
                then(dve.memset(per_e(0)[:, 0:1], 0.0))
                then(dve.tensor_tensor_scan(per_e(1), const("ones")[:, 0:EXPERTS], per_e(0), 0.0, ALU.mult, ALU.add))
                then(dve.tensor_tensor(per_e(2), per_e(1), per_e(0), ALU.subtract))
                then(dve.tensor_scalar(per_e(3), per_e(2), float(P), None, ALU.mult))
                then(dve.tensor_tensor(by_expert(before), by_expert(before), per_e(3).unsqueeze(2).to_broadcast([P, EXPERTS, TILES]), ALU.add))
                then(dve.tensor_tensor(by_tile(scratch), bank[0][:, 0:TE].rearrange("p (t e) -> p t e", e=EXPERTS),
                                       before.rearrange("p (e t) -> p t e", t=TILES), ALU.add))
                then(dve.tensor_tensor(scratch, scratch, onehot, ALU.mult))
                then(dve.reduce_sum(top, by_tile(scratch), axis=AX.X))
                then(dve.tensor_scalar(pick, by_tile(onehot)[:, :, 0], float(GROUPS * P), None, ALU.mult))
                then(dve.tensor_tensor(top, top, pick, ALU.add))
                dve.tensor_copy(SLOT[:, :], top).then_inc(slots_ready, 1)

            def group_experts():
                cmp = GCMP[0:1, :].rearrange("p (g e) -> p g e", e=EXPERTS)
                then(dve.tensor_tensor(cmp, per_e(1)[0:1, :].unsqueeze(1).to_broadcast([1, GROUPS, EXPERTS]),
                                       const("groups", 1).unsqueeze(2).to_broadcast([1, GROUPS, EXPERTS]), ALU.is_le))
                then(dve.reduce_sum(SMALL[0:1, 8 * TILES:8 * TILES + GROUPS], cmp, axis=AX.X))
                dve.tensor_scalar(GROUP_EXPERT[0:1, :], SMALL[0:1, 8 * TILES:8 * TILES + GROUPS], float(EXPERTS - 1), None,
                                  ALU.min).then_inc(groups_ready, 1)

            def copy_w1(n, par, guard):
                expert = dve.value_load(GROUP_EXPERT[0:1, bass.ds(n, 1)], min_val=0, max_val=EXPERTS - 1)
                if guard:
                    dve.wait_ge(f1_done, 2 * (TILES + n - 1))
                cols = bass.ds(expert * DFF, DFF)
                dve.tensor_copy(W1R[par][:, 0:DFF], W1A[:, cols])
                dve.tensor_copy(W1R[par][0:DB + 1, DFF:2 * DFF], W1B[0:DB + 1, cols]).then_inc(w1_copied, 1)

            def base(t):
                if t >= 4:
                    dve.wait_ge(out_stored[t % 4], 16 * (t // 4))
                dve.scalar_tensor_tensor(out=BASE[t % 4].rearrange("p (g n) -> p g n", g=2),
                                         in0=COMMON[:, :, t * (D // 2):(t + 1) * (D // 2)], scalar=KEEP1[:, t:t + 1],
                                         in1=H[:, t * D:t * D + D].rearrange("p (g n) -> p g n", g=2),
                                         op0=ALU.mult, op1=ALU.add).then_inc(base_ready, 1)

            def after_routing(s):
                if s == TILES + 3:
                    dve.wait_ge(groups_ready, 1)
                    dve.wait_ge(packed_zeroed, 16)
                    for n in range(2):
                        copy_w1(n, n, False)
                if s >= TILES + 4:
                    saved = s - AHEAD - 1
                    dve.wait_ge(y_used, saved)
                    first = 4 * (s - TILES - 4) if s < TILES + 8 else saved - 1
                    for t in range(first, min(first + 4, saved)):
                        base(t)

            dve.wait_ge(h_plus_xn, TILES)
            dve.wait_ge(mixer_w_in, 16 * 5)
            dve.wait_ge(o_copied, STEPS + 2)
            for par in range(2):
                dve.memset(OR[par][DB:DB + 1, P:2 * P], 1.0).then_inc(set_up, 1)
                dve.memset(XTF[par][DB:DB + 1, P:2 * P], 1.0).then_inc(set_up, 1)
            two_by_two(dve, mixer_step, (0, 2, AHEAD + 2), TILES, after_routing)


            def group_step(i, ks):
                kw, kh = ks
                if kw is not None:
                    n, par, half = tile_at(i, kw)
                    copy_w1(n, par, True)
                if kh is not None:
                    n, par, half = tile_at(i, kh)
                    expert = dve.value_load(GROUP_EXPERT[0:1, bass.ds(n, 1)], min_val=0, max_val=EXPERTS - 1)
                    dve.wait_ge(y_done, TILES + n + 1)
                    if kh >= 2:
                        dve.wait_ge(y_added[par], 16 * half)
                    dve.tensor_tensor(YR[par], bank[5 + par][:, 0:D], B2[:, bass.ds(expert * D, D)], ALU.add).then_inc(y_used, 1)
                    dve.wait_ge(y_used, TILES + n + 1)
                    if kh == 0:
                        dve.wait_ge(slot_rows_in, 16)
                    dve.tensor_scalar(YR[par], YR[par], SLOT_ROWS[:, bass.ds(n * 2, 1)], None, ALU.mult).then_inc(y_scaled, 1)

            two_by_two(dve, group_step, (0, 2), GROUPS, start=2)

        @block.gpsimd
        def _(pool):
            pool.memset(NEGHALF[:, :], -0.5).then_inc(zeroed, 1)
            def add_bias(t0, t1):
                h = H[:, t0 * D:t1 * D].rearrange("p (t d) -> p t d", d=D)
                pool.tensor_tensor(h, h, CB[:, :].unsqueeze(1).to_broadcast([P, t1 - t0, D]), ALU.add).then_inc(h_set, 1)

            pool.wait_ge(pos_in[0], 32)
            add_bias(0, 2)

            def spread(p, par, k):
                a = 2 * p + par
                if k >= 1:
                    pool.wait_ge(scores_done, a - 1)
                width = HEADS_A * SEQ
                for n in range(STEP_IMAGES):
                    pool.tensor_tensor(KR[par][:, n * width:(n + 1) * width].rearrange("p (h q) -> p h q", q=SEQ),
                                       KA[:, bass.ds(a * STEP_TOKENS + n * SEQ, SEQ)].unsqueeze(1).to_broadcast([P, HEADS_A, SEQ]),
                                       GM[:, 0:HEADS_A].unsqueeze(2).to_broadcast([P, HEADS_A, SEQ]), ALU.mult)
                base, hb = STEP_IMAGES * width, HEADS - HEADS_A
                for n in range(STEP_IMAGES):
                    last = pool.tensor_tensor(KR[par][0:DB, base + n * hb * SEQ:base + (n + 1) * hb * SEQ].rearrange("p (h q) -> p h q", q=SEQ),
                                              KB[0:DB, bass.ds(a * STEP_TOKENS + n * SEQ, SEQ)].unsqueeze(1).to_broadcast([DB, hb, SEQ]),
                                              GM[0:DB, HEADS_A:HEADS].unsqueeze(2).to_broadcast([DB, hb, SEQ]), ALU.mult)
                last.then_inc(kr_ready, 1)

            def patch_step(i, ks):
                kh, kq, kx, k_spread = ks
                if kx is not None:
                    t, par, half = tile_at(i, kx)
                    pool.wait_ge(xn_ready, t + 1)
                    h = H[:, bass.ds(t * D, D)]
                    pool.tensor_tensor(h, h, XN[par], ALU.add).then_inc(h_plus_xn, 1)
                if k_spread is not None:
                    p = tile_at(i, k_spread)[0]
                    if k_spread == 0:
                        pool.wait_ge(gains_ready, 1)
                    pool.wait_ge(qkT_copied, p + 3)
                    spread(p, 0, k_spread)
                if kh is not None:
                    t, par, half = tile_at(i, kh)
                    if kh >= 1:
                        pool.wait_ge(h_rstd, t)
                    pool.wait_ge(h_aggr, t + 1)
                    ride(pool)
                    pool.tensor_scalar(VE[:, 0:1], MVH[par][:, 1:2], EPS, None, ALU.add).then_inc(ve_h, 1)
                    pool.wait_ge(ve_h, t + 1)
                    pool.tensor_tensor(RSH[par][:, :], VE[:, 0:1], NEGHALF[:, 0:1], ALU.pow).then_inc(h_rstd, 1)
                if kq is not None:
                    t, par, half = tile_at(i, kq)
                    if kq >= 1:
                        pool.wait_ge(qk_rstd, t)
                    pool.wait_ge(qk_aggr, t + 1)
                    ride(pool)
                    pool.tensor_scalar(VE[:, 1:3], MVQK[par].rearrange("p (j s) -> p j s", s=2)[:, :, 1], EPS, None, ALU.add).then_inc(ve_qk, 1)
                    pool.wait_ge(ve_qk, t + 1)
                    pool.tensor_tensor(RSQK[par][:, :], VE[:, 1:3], NEGHALF[:, 0:2], ALU.pow).then_inc(qk_rstd, 1)
                if k_spread is not None:
                    spread(tile_at(i, k_spread)[0], 1, k_spread)
                if kh is not None and kh <= 7:
                    t = 2 * kh + 2
                    for part in (1, 2):
                        if t == ROW_PARTS[part][0]:
                            pool.wait_ge(pos_in[part], 16)
                    add_bias(t, t + 2)

            two_by_two(pool, patch_step, (0, 2, 1, SPREAD_LAG), TILES, counts=(TILES,) * 3 + (PAIR_STEPS,))

            def zero_packed():
                zeros = KR[0][:, 0:ROW]
                pool.wait_ge(scores_done, STEPS)
                pool.memset(zeros[:, 0:D + 1], 0.0).then_inc(zeroed, 1)
                pool.memset(zeros[:, D + 1:ROW].bitcast(I32), TOKENS).then_inc(zeroed, 1)
                pool.wait_ge(zeroed, 3)
                pool.dma_start(packed.rearrange("(g p) d -> p g d", p=P),
                               zeros.unsqueeze(1).to_broadcast([P, GROUPS, ROW])).then_inc(packed_zeroed, 16)

            def mixer_step(i, ks):
                kh, kf = ks
                if kh is not None:
                    t, par, half = tile_at(i, kh)
                    if kh >= 1:
                        pool.wait_ge(h2_rstd, t)
                    pool.wait_ge(h2_aggr, t + 1)
                    ride(pool)
                    pool.tensor_scalar(VE[:, 0:1], MVH[par][:, 1:2], EPS, None, ALU.add).then_inc(ve_h, 1)
                    pool.wait_ge(ve_h, TILES + t + 1)
                    pool.tensor_tensor(RSH[par][:, :], VE[:, 0:1], NEGHALF[:, 0:1], ALU.pow).then_inc(h2_rstd, 1)
                    pool.wait_ge(xn2_ready, t + 1)
                    pool.tensor_copy(XN2[:, bass.ds(t * ROW, D)], XR[par]).then_inc(xn2_saved, 1)
                if kh == 3:
                    zero_packed()
                if kf is not None:
                    t, par, half = tile_at(i, kf)
                    pool.wait_ge(xn2_saved, t + 1)
                    if kf >= 2:
                        pool.wait_ge(ffn_t_done, t - 1)
                    pool.tensor_copy(XF[par][:, 0:D], XN2[:, bass.ds(t * ROW, D)]).then_inc(xf_copied, 1)

            two_by_two(pool, mixer_step, (0, AHEAD - 1), TILES, counts=(TILES, XF_TILES))

            pool.wait_ge(packed_zeroed, 16)
            pool.wait_ge(slots_ready, 1)
            pool.wait_ge(rows_tagged, 1)
            for t in range(TILES):
                pool.indirect_dma_start(packed, bass.IndirectOffsetOnAxis(ap=SLOT[:, t:t + 1], axis=0),
                                        XN2[:, t * ROW:(t + 1) * ROW], None,
                                        bounds_check=GROUPS * P - 1, oob_is_err=False).then_inc(scattered, 16)

            def group_step(i, ks):
                kh, = ks
                n, par, half = tile_at(i, kh)
                if kh >= 2:
                    pool.wait_ge(y_added[par], 16 * half)
                pool.tensor_copy(ID[par][:, :], SLOT_ROWS[:, bass.ds(2 * n + 1, 1)].bitcast(I32)).then_inc(id_ready, 1)
                pool.wait_ge(id_ready, n + 1)
                pool.wait_ge(y_scaled, n + 1)
                if kh >= 1:
                    pool.wait_ge(y_added[1 - par], 16 * (half + par))
                ride(pool)
                pool.indirect_dma_start(out, bass.IndirectOffsetOnAxis(ap=ID[par][:, 0:1], axis=0), YR[par], None,
                                        bounds_check=TOKENS - 1, oob_is_err=False,
                                        compute_op=ALU.add).then_inc(y_added[par], 16)

            pool.wait_ge(slot_rows_in, 16)
            for ring4 in range(4):
                pool.wait_ge(out_stored[ring4], 16 * len(range(ring4, TILES, 4)))
            two_by_two(pool, group_step, (0,), GROUPS)


def _consts(np):
    c = np.zeros((P, NCONST), np.float32)

    def put(name, value):
        a, b = CONSTS[name]
        c[:, a:b] = value

    put("ident", np.eye(P))
    put("before", np.triu(np.ones((P, P)), 1))
    put("ones", 1.0)
    put("first", np.arange(EXPERTS, 0, -1))
    put("thresholds", np.arange(TILES) * P)
    put("groups", np.arange(GROUPS))
    put("keep", np.tile(np.arange(TILES) > 0, EXPERTS))
    row = np.arange(P)[:, None]
    put("heads_a", row // HD == np.arange(HEADS_A))
    put("heads_b", row // HD == np.arange(HEADS - HEADS_A))
    put("parity", row // SEQ == np.arange(2))
    return c


def _position_rows(np):
    edges = np.arange(1.0 / POS_TABLE_SIDE, 1.0, 1.0 / POS_TABLE_SIDE, dtype=np.float32)
    at = np.searchsorted(edges, np.arange(0.0, 1.0 - 1e-06, 1.0 / GRID, dtype=np.float32), side="right")
    return (at[:, None] * POS_TABLE_SIDE + at).reshape(-1)


def kernel(**inputs):
    import numpy as np
    import concourse.bacc as _bacc
    from concourse.bass_utils import run_bass_kernel_spmd as _run

    g = {k: np.asarray(v) for k, v in inputs.items()}

    def with_row(w, b):
        return np.concatenate([w, b[None]], axis=0)

    x = g["x"].reshape(IMAGES, CHANNELS, GRID, PATCH, GRID, PATCH).transpose(1, 3, 5, 0, 2, 4)
    x = x.reshape(KC, P, TILES, P).transpose(2, 1, 0, 3).reshape(TILES, P, KC * P)
    zero = np.zeros((D,), np.float32)
    w_qkv = np.concatenate([with_row(g["L0_attn_Wq"].T, zero), with_row(g["L0_attn_Wk"].T, g["L0_attn_bk"]),
                            with_row(g["L0_attn_Wv"].T, g["L0_attn_bv"])], axis=1)
    pos = g["L0_tok_pos_table"][_position_rows(np)]
    pos = np.tile(pos, (IMAGES, 1)).reshape(TILES, P, D).transpose(1, 0, 2).reshape(P, TILES * D)
    w1 = g["L0_ffn_W1"].transpose(1, 0, 2).reshape(D, EXPERTS * DFF)
    arrays = {
        "patches": x,
        "conv_w": g["L0_tok_conv_w"].reshape(D, KC, P).transpose(2, 1, 0).reshape(P, KC * D),
        "conv_b": np.tile(g["L0_tok_conv_b"], (P, 1)),
        "pos": pos,
        "w_qkv": w_qkv,
        "w_o": with_row(g["L0_attn_Wo"].T, g["L0_attn_bo"]),
        "gq": g["L0_attn_gq"][:, None],
        "gk": g["L0_attn_gk"][:, None],
        "w_router": with_row(g["L0_ffn_Ws"], g["L0_ffn_bs"]),
        "w1": w1[0:P],
        "w1_rest": with_row(w1[P:D], g["L0_ffn_b1"].reshape(-1)),
        "w2": g["L0_ffn_W2"].reshape(EXPERTS, FC, P, D).transpose(2, 0, 1, 3).reshape(P, EXPERTS * FC * D),
        "b2": np.tile(g["L0_ffn_b2"].reshape(1, -1), (P, 1)),
        "consts": _consts(np),
        "ids": np.arange(TOKENS, dtype=np.int32).reshape(TILES, P).T,
    }
    arrays = {f"in_{k}": np.ascontiguousarray(v) for k, v in arrays.items()}
    nc = _bacc.Bacc("TRN2", target_bir_lowering=False, num_devices=1)
    args = [nc.dram_tensor(k, v.shape, mybir.dt.from_np(v.dtype), kind="ExternalInput").ap() for k, v in arrays.items()]
    out = nc.dram_tensor("out", (TOKENS, D), F32, kind="ExternalOutput").ap()
    vit_kernel(nc, *args, out)
    r = _run(nc, [arrays], core_ids=[0])
    return r.results[0]["out"].reshape(IMAGES, SEQ, D)
```

```python
from contextlib import ExitStack

import concourse.bass as bass
from concourse import mybir

F32 = mybir.dt.float32
I32 = mybir.dt.int32
ALU = mybir.AluOpType
ACT = mybir.ActivationFunctionType
AX = mybir.AxisListType

P = 128
IMAGES, CHANNELS, SIDE = 64, 3, 96
PATCH = 16
GRID = SIDE // PATCH
SEQ = GRID * GRID
TOKENS = IMAGES * SEQ
TILES = TOKENS // P
D = 192
DB = D - P
PIXELS = CHANNELS * PATCH * PATCH
KC = PIXELS // P
HEADS, HD = 12, 16
HEADS_A = P // HD
PAIRS = HEADS // 2
DFF = 768
FC = DFF // P
FH = DFF // 2
EXPERTS = 9
EPS = 1e-5
GROUPS = (TOKENS + (EXPERTS - 1) * (P - 1)) // P
AHEAD = 10
EARLY_ROWS = 4
ROW = D + 2
STEP_IMAGES = 2
ROW_PARTS = ((0, 2), (2, 8), (8, TILES))
STEPS = IMAGES // STEP_IMAGES
BASES_FIRST = 12
PAIR_STEPS = STEPS // 2
SPREAD_LAG, SCORE_LAG, WEIGH_LAG = 6, 7, 8
MIXER_START = TILES + 2
PATCH_END = WEIGH_LAG + PAIR_STEPS
STEP_TOKENS = STEP_IMAGES * SEQ
K2 = 2 * SEQ
TE = TILES * EXPERTS
POS_TABLE_SIDE = 32

CONSTS = {}
_at = 0
for _name, _n in (("ident", P), ("before", P), ("ones", P), ("first", EXPERTS), ("thresholds", TILES),
                  ("groups", GROUPS), ("keep", TE), ("heads_a", HEADS_A), ("heads_b", HEADS - HEADS_A),
                  ("parity", 2)):
    CONSTS[_name] = (_at, _at + _n)
    _at += _n
NCONST = _at


def tile_at(i, k):
    return 2 * i + k, k % 2, i + k // 2


def vit_kernel(nc, patches, conv_w, conv_b, pos, w_qkv, w_o, gq, gk, w_router, w1, w1_rest, w2, b2, consts, ids, out):
    packed = nc.dram_tensor("packed_tokens", (GROUPS * P, ROW), F32, kind="Internal").ap()
    v_dram = nc.dram_tensor("v_rows", (TOKENS, D), F32, kind="Internal").ap()
    v_by_image = v_dram.rearrange("(n k) d -> k n d", k=SEQ)

    with ExitStack() as ctx:
        def sb(name, cols, dt=F32):
            return ctx.enter_context(nc.sbuf_tensor(name, [P, cols], dt))

        def sem(name):
            return ctx.enter_context(nc.semaphore(name))

        bank = [ctx.enter_context(nc.psum_tensor(f"bank{i}", [P, 512], F32)) for i in range(8)]

        W1A = sb("W1A", EXPERTS * DFF)
        W1B = sb("W1B", EXPERTS * DFF)
        W2 = sb("W2", EXPERTS * FC * D)
        B2 = sb("B2", EXPERTS * D)
        H = sb("H", TILES * D)
        QK = sb("QK", 4 * TOKENS)
        CST = sb("CST", NCONST)
        WO = sb("WO", 2 * D)
        WR = sb("WR", 2 * EXPERTS)
        NEGHALF = sb("NEGHALF", 2)
        LOG = sb("LOG", TE)
        KEEP1 = sb("KEEP1", TILES)
        SHARE = sb("SHARE", TILES)
        SLOT = sb("SLOT", TILES, I32)
        IDS = sb("IDS", TILES, I32)
        SLOT_ROWS = sb("SLOT_ROWS", 2 * GROUPS)
        ID = [sb(f"ID{i}", 1, I32) for i in range(2)]
        GROUP_EXPERT = sb("GROUP_EXPERT", GROUPS, I32)

        def const(name, rows=P):
            a, b = CONSTS[name]
            return CST[0:rows, a:b]

        ARENA = sb("ARENA", 5800)
        marks = [0]

        def cut(n):
            a = marks[0]
            marks[0] += n
            assert marks[0] <= 5800
            return ARENA[:, a:a + n]

        PT = [cut(KC * P) for _ in range(2)]
        CW = cut(KC * D)
        WQKV = [cut(3 * D) for _ in range(2)]
        XN = [cut(D) for _ in range(2)]
        QKN = [cut(2 * D) for _ in range(2)]
        VST = [cut(D) for _ in range(2)]
        marks[0] = 0
        HT = [cut(DFF) for _ in range(2)]
        XR = [cut(D) for _ in range(2)]
        at = marks[0]
        XF = [cut(ROW) for _ in range(2)]
        YR = [cut(D) for _ in range(2)]
        cut(EARLY_ROWS * ROW - 2 * (ROW + D))
        XN2_EARLY = ARENA[:, at:at + EARLY_ROWS * ROW]
        OR = [cut(2 * P) for _ in range(2)]
        BASE = [cut(D) for _ in range(4)]
        RT = cut(8 * TE)

        RINGS = sb("RINGS", 3600)

        def ring(at, n):
            return [RINGS[:, at + i * n:at + (i + 1) * n] for i in range(2)]

        nk, ns = STEP_IMAGES * HEADS * SEQ, STEP_IMAGES * PAIRS * SEQ
        KR = ring(0, nk)
        SB = ring(2 * nk, ns)
        PR = ring(2 * (nk + ns), ns)
        W1R = ring(0, 2 * DFF)
        XTF = ring(4 * DFF, 2 * P)

        XT = [sb(f"XT{i}", 2 * P) for i in range(2)]
        V2 = [sb(f"V2{i}", STEP_IMAGES * D) for i in range(2)]
        VS = [sb(f"VS{i}", STEP_IMAGES * D) for i in range(2)]
        NP2 = STEP_IMAGES * PAIRS
        MX = sb("MX", NP2)
        SM = sb("SM", NP2)
        RC = sb("RC", NP2)
        R2 = sb("R2", 2 * NP2)
        GAIN = sb("GAIN", 4)
        GM = sb("GM", HEADS)
        STH = sb("STH", 6)
        STQK = sb("STQK", 12)
        MVH = [sb(f"MVH{i}", 2) for i in range(2)]
        MVQK = [sb(f"MVQK{i}", 4) for i in range(2)]
        RSH = [sb(f"RSH{i}", 1) for i in range(2)]
        RSQK = [sb(f"RSQK{i}", 2) for i in range(2)]
        VE = sb("VE", 3)
        CB = sb("CB", D)
        SMALL = sb("SMALL", 16 * TILES)
        SMALLE = sb("SMALLE", 8 * EXPERTS)
        GCMP = sb("GCMP", GROUPS * EXPERTS)

        QA, QB = QK[:, 0:TOKENS], QK[:, TOKENS:2 * TOKENS]
        KA, KB = QK[:, 2 * TOKENS:3 * TOKENS], QK[:, 3 * TOKENS:4 * TOKENS]
        XN2T = QK[:, 2 * TOKENS:4 * TOKENS]
        XN2_LATE = RINGS[:, 0:(TILES - EARLY_ROWS) * ROW]
        assert 2 * P * TILES == 2 * TOKENS and (TILES - EARLY_ROWS) * ROW < 4 * DFF
        COMMON = QK[:, 0:2 * TOKENS].rearrange("p (g n) -> p g n", g=2)

        def xn2_rows(t):
            if t < EARLY_ROWS:
                return XN2_EARLY[:, t * ROW:(t + 1) * ROW]
            return XN2_LATE[:, (t - EARLY_ROWS) * ROW:(t - EARLY_ROWS + 1) * ROW]

        consts_in = sem("consts_in")
        pos_in = [sem(f"pos_in{i}") for i in range(3)]
        gains_in = sem("gains_in")
        conv_w_in = sem("conv_w_in")
        qkv_w_in = sem("qkv_w_in")
        mixer_w_in = sem("mixer_w_in")
        expert_w_in = sem("expert_w_in")
        patch_in = [sem(f"patch_in{i}") for i in range(2)]
        gains_ready = sem("gains_ready")
        set_up = sem("set_up")
        h_set = sem("h_set")
        conv_done = sem("conv_done")
        h_added = sem("h_added")
        h_stats = sem("h_stats")
        h_aggr = sem("h_aggr")
        h_rstd = sem("h_rstd")
        xn_ready = sem("xn_ready")
        h_plus_xn = sem("h_plus_xn")
        xt_transposed = sem("xt_transposed")
        xt_copied = sem("xt_copied")
        qk_done = sem("qk_done")
        v_done = sem("v_done")
        v_copied = sem("v_copied")
        v_stored = [sem(f"v_stored{i}") for i in range(2)]
        qk_stats = sem("qk_stats")
        qk_aggr = sem("qk_aggr")
        qk_rstd = sem("qk_rstd")
        qk_normed = sem("qk_normed")
        qkT_done = sem("qkT_done")
        qkT_copied = sem("qkT_copied")
        waited = sem("waited")
        ve_h = sem("ve_h")
        ve_qk = sem("ve_qk")
        kr_ready = sem("kr_ready")
        scores_done = sem("scores_done")
        max_ready = sem("max_ready")
        s_shifted = sem("s_shifted")
        exp_done = sem("exp_done")
        denom = sem("denom")
        v2_in = [sem(f"v2_in{i}") for i in range(2)]
        vs_ready = sem("vs_ready")
        pv_done = sem("pv_done")
        o_copied = sem("o_copied")
        or_ready = sem("or_ready")
        w_done = sem("w_done")
        h2_added = sem("h2_added")
        h2_stats = sem("h2_stats")
        h2_aggr = sem("h2_aggr")
        h2_rstd = sem("h2_rstd")
        xn2_ready = sem("xn2_ready")
        xn2_saved = sem("xn2_saved")
        ffn_t_done = sem("ffn_t_done")
        ffn_xt = sem("ffn_xt")
        f1_done = sem("f1_done")
        gelu_done = sem("gelu_done")
        w1_copied = sem("w1_copied")
        xt1_done = sem("xt1_done")
        xt1_copied = sem("xt1_copied")
        xn2t_saved = sem("xn2t_saved")
        y_done = sem("y_done")
        y_used = sem("y_used")
        router_done = sem("router_done")
        log_copied = sem("log_copied")
        rt = sem("rt")
        log_shifted = sem("log_shifted")
        log_exp = sem("log_exp")
        chosen = sem("chosen")
        ranks_done = sem("ranks_done")
        slots_ready = sem("slots_ready")
        groups_ready = sem("groups_ready")
        zeroed = sem("zeroed")
        packed_zeroed = sem("packed_zeroed")
        scattered = sem("scattered")
        xr_in = [sem(f"xr_in{i}") for i in range(2)]
        rows_tagged = sem("rows_tagged")
        slot_rows_in = sem("slot_rows_in")
        id_ready = sem("id_ready")
        y_biased = sem("y_biased")
        y_scaled = sem("y_scaled")
        y_added = [sem(f"y_added{i}") for i in range(2)]
        base_ready = sem("base_ready")
        out_stored = [sem(f"out_stored{i}") for i in range(4)]

        def ride(e):
            e.sem_inc(waited, 1)

        def stages(s, lags, counts):
            return [s - lag if 0 <= s - lag < count else None for lag, count in zip(lags, counts)]

        def two_by_two(e, step, lags, tiles, after=None, counts=None, start=0, outside=0):
            counts = counts or [tiles] * len(lags)
            last = max(lags)
            end = max(lag + count for lag, count in zip(lags, counts))
            first = max(last + 2, outside)
            first += (tiles - first) % 2
            assert start <= first < tiles <= min(lag + count for lag, count in zip(lags, counts))

            for s in range(start, first):
                step(0, stages(s, lags, counts))
            with e.Fori(0, (tiles - first) // 2) as i:
                for u in range(2):
                    step(i, [first + u - lag for lag in lags])
            for s in range(tiles, end):
                step(0, stages(s, lags, counts))
                if after:
                    after(s)

        block = ctx.enter_context(nc.Block())

        @block.sync
        def _(sp):
            def h_rows(t0, t1):
                return slice(t0 * D, t1 * D)

            def load_rows(part):
                t0, t1 = ROW_PARTS[part]
                sp.dma_start(H[:, h_rows(t0, t1)], pos[:, h_rows(t0, t1)]).then_inc(pos_in[part], 16)

            sp.dma_start(PT[0], patches[0]).then_inc(patch_in[0], 16)
            sp.dma_start(CW, conv_w).then_inc(conv_w_in, 16)
            sp.dma_start(CB[:], conv_b).then_inc(pos_in[0], 16)
            load_rows(0)
            sp.dma_start(PT[1], patches[1]).then_inc(patch_in[1], 16)
            sp.dma_start(CST[:], consts).then_inc(consts_in, 16)
            sp.dma_start(WQKV[0], w_qkv[0:P]).then_inc(qkv_w_in, 16)
            sp.dma_start(WQKV[1][0:DB + 1], w_qkv[P:D + 1]).then_inc(qkv_w_in, 16)
            load_rows(1)

            def load_patch(t, par):
                sp.wait_ge(conv_done, t - 1)
                sp.dma_start(PT[par], patches[bass.ds(t, 1)].rearrange("a p n -> (a p) n")).then_inc(patch_in[par], 16)

            def store_v(t, par):
                sp.wait_ge(v_copied, t + 1)
                sp.dma_start(v_dram[bass.ds(t * P, P)], VST[par]).then_inc(v_stored[par], 16)

            def load_up(e):
                cols = bass.ds(e * DFF, DFF)
                sp.dma_start(W1A[:, cols], w1[:, cols]).then_inc(expert_w_in, 16)
                sp.dma_start(W1B[0:DB + 1, cols], w1_rest[:, cols]).then_inc(expert_w_in, 16)

            def load_down(e):
                cols = bass.ds(e * FC * D, FC * D)
                sp.dma_start(W2[:, cols], w2[:, cols]).then_inc(expert_w_in, 16)

            def v2_load(p, i, k):
                sp.wait_ge(v_stored[0], 16 * (i + (k + 2) // 2 + 1))
                sp.wait_ge(v_stored[1], 16 * (i + (k + 1) // 2 + 1))
                for par in range(2):
                    a = 2 * p + par
                    if k >= 1:
                        sp.wait_ge(vs_ready, a - 1)
                    for copy in range(2):
                        sp.dma_start(V2[par][copy * SEQ:copy * SEQ + SEQ, :].rearrange("p (n d) -> p n d", n=STEP_IMAGES),
                                     v_by_image[:, bass.ds(a * STEP_IMAGES, STEP_IMAGES), :]).then_inc(v2_in[par], 16)

            def load_step(i, ks):
                kp, kv, k2, ke = ks
                if kp == 4:
                    load_rows(2)
                    for row, g in enumerate((gq, gk)):
                        sp.dma_start(GAIN[:, row:row + 1], g[0:P]).then_inc(gains_in, 16)
                        sp.dma_start(GAIN[0:DB, 2 + row:3 + row], g[P:D]).then_inc(gains_in, 16)
                if kp == 7:
                    for dst, src in ((WO[:, 0:D], w_o[0:P]), (WO[0:DB + 1, D:2 * D], w_o[P:D + 1]),
                                     (WR[:, 0:EXPERTS], w_router[0:P]), (WR[0:DB + 1, EXPERTS:2 * EXPERTS], w_router[P:D + 1])):
                        sp.dma_start(dst, src).then_inc(mixer_w_in, 16)
                    sp.dma_start(IDS[:], ids).then_inc(mixer_w_in, 16)
                if kp is not None and kp >= 2:
                    t, par, half = tile_at(i, kp)
                    load_patch(t, par)
                if kv is not None:
                    t, par, half = tile_at(i, kv)
                    store_v(t, par)
                if k2 is not None:
                    v2_load(tile_at(i, k2)[0], i, k2)
                if ke is not None:
                    load_up(tile_at(i, ke)[0])
                    load_down(tile_at(i, ke)[0])

            two_by_two(sp, load_step, (0, 4, SPREAD_LAG + 2, TILES - EXPERTS), TILES,
                       counts=(TILES, TILES, PAIR_STEPS, EXPERTS))
            sp.dma_start(B2[:], b2).then_inc(expert_w_in, 16)

            def store_base(t):
                sp.wait_ge(base_ready, t + 1)
                sp.dma_start(out[t * P:t * P + P], BASE[t % 4]).then_inc(out_stored[t % 4], 16)

            for t in range(BASES_FIRST):
                store_base(t)
            sp.wait_ge(scattered, 16 * TILES)
            for r in range(2):
                sp.dma_start(XF[r], packed[r * P:r * P + P]).then_inc(xr_in[r], 16)
            sp.dma_start(SLOT_ROWS[:, :].rearrange("p (g w) -> p g w", w=2),
                         packed.rearrange("(g p) w -> p g w", p=P)[:, :, D:ROW]).then_inc(slot_rows_in, 16)
            for t in range(BASES_FIRST, TILES):
                store_base(t)

            def load_group(i, ks):
                n, par, half = tile_at(i, ks[0])
                sp.wait_ge(ffn_t_done, n - 1)
                sp.dma_start(XF[par], packed[bass.ds(n * P, P)]).then_inc(xr_in[par], 16)

            two_by_two(sp, load_group, (0,), GROUPS, start=2)
            for ring4 in range(4):
                sp.wait_ge(out_stored[ring4], 16 * len(range(ring4, TILES, 4)))
            for par in range(2):
                sp.wait_ge(y_added[par], 16 * len(range(par, GROUPS, 2)))

        @block.tensor
        def _(pe):
            ident = const("ident")

            def conv(i, k):
                t, par, half = tile_at(i, k)
                pe.wait_ge(patch_in[par], 16 * (half + 1))
                if k >= 1:
                    pe.wait_ge(h_added, t)
                for c in range(KC):
                    last = pe.matmul(bank[0][:, 0:D], PT[par][:, c * P:c * P + P], CW[:, c * D:c * D + D],
                                     start=c == 0, stop=c == KC - 1)
                last.then_inc(conv_done, 1)

            def transpose_tile(src, dst):
                pe.transpose(dst[:, 0:P], src[:, 0:P], ident)
                return pe.transpose(dst[0:DB, P:2 * P], src[:, P:D], ident)

            def transpose_xn(i, k):
                t, par, half = tile_at(i, k)
                pe.wait_ge(xn_ready, t + 1)
                if k == 0:
                    pe.wait_ge(consts_in, 16)
                if k >= 3:
                    pe.wait_ge(qkT_copied, t - 2)
                transpose_tile(XN[par], bank[1]).then_inc(xt_transposed, 1)

            def project(i, k):
                t, par, half = tile_at(i, k)
                pe.wait_ge(xt_copied, t + 1)
                if k == 0:
                    pe.wait_ge(qkv_w_in, 32)
                    pe.wait_ge(set_up, 2)
                if k >= 1:
                    pe.wait_ge(qk_normed, t)
                x = XT[par]
                pe.matmul(bank[2][:, 0:2 * D], x[:, 0:P], WQKV[0][:, 0:2 * D], start=True, stop=False)
                pe.matmul(bank[2][:, 0:2 * D], x[0:DB + 1, P:2 * P], WQKV[1][0:DB + 1, 0:2 * D], start=False, stop=True).then_inc(qk_done, 1)
                if k >= 1:
                    pe.wait_ge(v_copied, t)
                pe.matmul(bank[3][:, 0:D], x[:, 0:P], WQKV[0][:, 2 * D:3 * D], start=True, stop=False)
                pe.matmul(bank[3][:, 0:D], x[0:DB + 1, P:2 * P], WQKV[1][0:DB + 1, 2 * D:3 * D], start=False, stop=True).then_inc(v_done, 1)

            def transpose_qk(i, k):
                t, par, half = tile_at(i, k)
                pe.wait_ge(qk_normed, t + 1)
                pe.wait_ge(xt_copied, min(t + 3, TILES) if isinstance(t, int) else t + 3)
                for j in range(3):
                    last = pe.transpose(bank[1][:, j * P:j * P + P], QKN[par][:, j * P:j * P + P], ident)
                last.then_inc(qkT_done, 1)

            def scores(p, par, k):
                a = 2 * p + par
                pe.wait_ge(kr_ready, a + 1)
                if k >= 1:
                    pe.wait_ge(s_shifted, a - 1)
                ka = KR[par][:, 0:STEP_IMAGES * HEADS_A * SEQ]
                kb = KR[par][0:DB, STEP_IMAGES * HEADS_A * SEQ:]
                for n in range(STEP_IMAGES):
                    for j in range(PAIRS):
                        if j < HEADS_A // 2:
                            at = n * HEADS_A * SEQ + j * K2
                            keys, queries = ka[:, at:at + K2], QA[:, bass.ds(a * STEP_TOKENS + n * SEQ, SEQ)]
                        else:
                            at = n * (HEADS - HEADS_A) * SEQ + (j - HEADS_A // 2) * K2
                            keys, queries = kb[:, at:at + K2], QB[0:DB, bass.ds(a * STEP_TOKENS + n * SEQ, SEQ)]
                        o = (n * PAIRS + j) * SEQ
                        last = pe.matmul(bank[4 + par][0:K2, o:o + SEQ], keys, queries, start=True, stop=True)
                last.then_inc(scores_done, 1)

            def weigh_v(p, par):
                a = 2 * p + par
                pe.wait_ge(vs_ready, a + 1)
                pe.wait_ge(o_copied, a + 1)
                for n in range(STEP_IMAGES):
                    for j in range(PAIRS):
                        at = n * PAIRS + j
                        row = 32 * (j % 4)
                        col = (j // 4) * STEP_TOKENS + n * SEQ
                        last = pe.matmul(bank[6 + par][row:row + 32, col:col + SEQ], VS[par][0:K2, at * 32:at * 32 + 32],
                                         PR[par][0:K2, at * SEQ:at * SEQ + SEQ], start=True, stop=True)
                last.then_inc(pv_done, 1)

            def patch_step(i, ks):
                kc, kq, kp, kx, k_scores, k_weigh = ks
                if kc is not None:
                    conv(i, kc)
                if k_scores is not None:
                    scores(tile_at(i, k_scores)[0], 0, k_scores)
                if k_weigh is not None:
                    weigh_v(tile_at(i, k_weigh)[0], 0)
                if kq is not None:
                    transpose_qk(i, kq)
                if k_scores is not None:
                    scores(tile_at(i, k_scores)[0], 1, k_scores)
                if kp is not None:
                    project(i, kp)
                if k_weigh is not None and k_weigh != PAIR_STEPS - 1:
                    weigh_v(tile_at(i, k_weigh)[0], 1)
                if kx is not None:
                    transpose_xn(i, kx)

            def project_o(i, k):
                t, par, half = tile_at(i, k)
                pe.wait_ge(or_ready, t + 1)
                if k == 0:
                    pe.wait_ge(mixer_w_in, 16 * 5)
                    pe.wait_ge(set_up, 4)
                    pe.wait_ge(h_added, TILES)
                if k >= 1:
                    pe.wait_ge(h2_added, t)
                o = OR[par]
                pe.matmul(bank[0][:, 0:D], o[:, 0:P], WO[:, 0:D], start=True, stop=False)
                pe.matmul(bank[0][:, 0:D], o[0:DB + 1, P:2 * P], WO[0:DB + 1, D:2 * D], start=False, stop=True).then_inc(w_done, 1)

            def ffn_up(n, x, first, rest, guard):
                for c in range(FC):
                    g, at = c // (FC // 2), c % (FC // 2) * P
                    if guard and at == 0:
                        pe.wait_ge(gelu_done, 2 * n - 1 + g)
                    pe.matmul(bank[3 + g][:, at:at + P], first[:, c * P:c * P + P], x[:, 0:P], start=True, stop=False)
                    last = pe.matmul(bank[3 + g][:, at:at + P], rest[0:DB + 1, c * P:c * P + P], x[0:DB + 1, P:2 * P],
                                     start=False, stop=True)
                    if c % (FC // 2) == FC // 2 - 1:
                        last.then_inc(f1_done, 1)

            def ffn_down(n, par, expert, guard):
                if guard:
                    pe.wait_ge(y_used, n - 1)
                for c in range(FC):
                    if c % (FC // 2) == 0:
                        pe.wait_ge(gelu_done, 2 * n + 1 + c // (FC // 2))
                    last = pe.matmul(bank[6 + par][:, 0:D], HT[par][:, c * P:c * P + P], W2[:, bass.ds((expert * FC + c) * D, D)],
                                     start=c == 0, stop=c == FC - 1)
                last.then_inc(y_done, 1)

            def route(t, par, guard):
                if guard:
                    pe.wait_ge(log_copied, t)
                else:
                    pe.wait_ge(qk_normed, TILES)
                x = XT[par]
                pe.matmul(bank[2][:, 0:EXPERTS], x[:, 0:P], WR[:, 0:EXPERTS], start=True, stop=False)
                pe.matmul(bank[2][:, 0:EXPERTS], x[0:DB + 1, P:2 * P], WR[0:DB + 1, EXPERTS:2 * EXPERTS],
                          start=False, stop=True).then_inc(router_done, 1)

            def transpose_group(i, k):
                n, par, half = tile_at(i, k)
                pe.wait_ge(xr_in[par], 16 * (half + 1))
                if k >= 1:
                    pe.wait_ge(ffn_xt, n)
                transpose_tile(XF[par], bank[5]).then_inc(ffn_t_done, 1)

            def mixer_step(i, ks):
                kw, k1, kr, kf, kh = ks
                if kf is not None:
                    t, par, half = tile_at(i, kf)
                    if kf == 0:
                        pe.wait_ge(v_copied, TILES)
                        pe.wait_ge(expert_w_in, 16 * (3 * EXPERTS + 1))
                        pe.wait_ge(o_copied, STEPS + 2)
                    pe.wait_ge(xn2t_saved, t + 1)
                    ffn_up(t, XN2T[:, bass.ds(t * 2 * P, 2 * P)], W1A, W1B, kf >= 1)
                if kw is not None:
                    project_o(i, kw)
                if kr is not None:
                    t, par, half = tile_at(i, kr)
                    pe.wait_ge(xt1_copied, t + 1)
                    route(t, par, kr >= 1)
                if kh == TILES - 1:
                    transpose_group(0, 0)
                if kh is not None:
                    t, par, half = tile_at(i, kh)
                    ffn_down(t, par, 0, kh >= 2)
                if kh == TILES - 1:
                    transpose_group(0, 1)
                if k1 is not None:
                    t, par, half = tile_at(i, k1)
                    pe.wait_ge(xn2_ready, t + 1)
                    if k1 >= 1:
                        pe.wait_ge(xn2t_saved, t)
                    else:
                        pe.wait_ge(qkT_copied, TILES)
                    transpose_tile(XR[par], bank[1]).then_inc(xt1_done, 1)

            def count_ranks(s):
                if s == TILES + 1:
                    pe.wait_ge(chosen, 1)
                    onehot = RT[:, 0:TE]
                    pe.wait_ge(h2_added, TILES)
                    pe.matmul(bank[0][:, 0:TE], const("before"), onehot, start=True, stop=True)
                    pe.matmul(bank[2][:, 0:TE], const("ones"), onehot, start=True, stop=True).then_inc(ranks_done, 1)

            mixer_lags = (0, 1, 2, AHEAD, AHEAD + 1)

            def mixer_beside(s):
                if s >= MIXER_START:
                    mixer_step(0, stages(s - MIXER_START, mixer_lags, [TILES] * 5))
                if s == PATCH_END - 1:
                    weigh_v(PAIR_STEPS - 1, 1)

            pe.sem_inc(qkT_done, 2)
            pe.wait_ge(conv_w_in, 16)
            two_by_two(pe, patch_step, (0, 4, 2, 1, SCORE_LAG, WEIGH_LAG), TILES,
                       counts=(TILES,) * 4 + (PAIR_STEPS,) * 2, after=mixer_beside)

            two_by_two(pe, mixer_step, mixer_lags, TILES, count_ranks, start=PATCH_END - MIXER_START)

            def group_step(i, ks):
                kt, kf, kh = ks
                if kf is not None:
                    n, par, half = tile_at(i, kf)
                    pe.wait_ge(w1_copied, n + 1)
                    pe.wait_ge(ffn_xt, n + 1)
                    ffn_up(TILES + n, XTF[par], W1R[par][:, 0:DFF], W1R[par][:, DFF:2 * DFF], True)
                if kt is not None and kt >= 2:
                    transpose_group(i, kt)
                if kh is not None:
                    n, par, half = tile_at(i, kh)
                    expert = pe.value_load(GROUP_EXPERT[0:1, bass.ds(n, 1)], min_val=0, max_val=EXPERTS - 1)
                    ffn_down(TILES + n, par, expert, True)

            pe.wait_ge(groups_ready, 1)
            pe.wait_ge(set_up, 6)
            two_by_two(pe, group_step, (0, 1, 2), GROUPS)

        @block.scalar
        def _(act):
            def copy_xt(dst, src):
                act.activation(dst[:, 0:P], src[:, 0:P], ACT.Copy)
                return act.activation(dst[0:DB, P:2 * P], src[0:DB, P:2 * P], ACT.Copy)

            def exp_scores(p, par, k):
                a = 2 * p + par
                act.wait_ge(s_shifted, a + 1)
                if k >= 1:
                    act.wait_ge(pv_done, a - 1)
                act.activation(PR[par][0:K2, :], SB[par][0:K2, :], ACT.Exp, scale=HD ** -0.5).then_inc(exp_done, 1)

            def copy_o(p, par):
                a = 2 * p + par
                act.wait_ge(pv_done, a + 1)
                act.activation(QA[:, bass.ds(a * STEP_TOKENS, STEP_TOKENS)], bank[6 + par][:, 0:STEP_TOKENS], ACT.Copy)
                act.activation(QB[0:DB, bass.ds(a * STEP_TOKENS, STEP_TOKENS)],
                               bank[6 + par][0:DB, STEP_TOKENS:2 * STEP_TOKENS], ACT.Copy).then_inc(o_copied, 1)

            def patch_step(i, ks):
                kx, kv, kq, k_exp, k_o = ks
                if k_exp is not None:
                    exp_scores(tile_at(i, k_exp)[0], 0, k_exp)
                if k_o is not None:
                    copy_o(tile_at(i, k_o)[0], 0)
                if kq is not None:
                    t, par, half = tile_at(i, kq)
                    act.wait_ge(qkT_done, t + 3)
                    qk = QK[:, :].rearrange("p (j g n) -> p j g n", j=2, g=2)
                    act.activation(qk[:, :, 0, bass.ds(t * P, P)],
                                   bank[1][:, 0:4 * P].rearrange("p (j n) -> p j n", j=2)[:, :, 0:P], ACT.Copy)
                    act.activation(QB[0:DB, bass.ds(t * P, P)], bank[1][0:DB, P:2 * P], ACT.Copy)
                    act.activation(KB[0:DB, bass.ds(t * P, P)], bank[1][DB:P, P:2 * P], ACT.Copy).then_inc(qkT_copied, 1)
                if k_exp is not None:
                    exp_scores(tile_at(i, k_exp)[0], 1, k_exp)
                if kv is not None:
                    t, par, half = tile_at(i, kv)
                    act.wait_ge(v_done, t + 1)
                    if kv >= 2:
                        act.wait_ge(v_stored[par], 16 * half)
                    act.activation(VST[par], bank[3][:, 0:D], ACT.Copy).then_inc(v_copied, 1)
                if k_o is not None:
                    copy_o(tile_at(i, k_o)[0], 1)
                if kx is not None:
                    t, par, half = tile_at(i, kx)
                    act.wait_ge(xt_transposed, t + 1)
                    if kx >= 2:
                        act.wait_ge(v_done, t - 1)
                    copy_xt(XT[par], bank[1]).then_inc(xt_copied, 1)

            def gelu(n, par, guard):
                for g in range(2):
                    act.wait_ge(f1_done, 2 * n + 1 + g)
                    if guard and g == 0:
                        act.wait_ge(y_done, n - 1)
                    act.activation(HT[par][:, g * FH:g * FH + FH], bank[3 + g][:, 0:FH], ACT.Gelu).then_inc(gelu_done, 1)

            def mixer_step(i, ks):
                ko, kx, kg = ks
                if kg is not None:
                    t, par, half = tile_at(i, kg)
                    gelu(t, par, kg >= 2)
                if ko is not None:
                    t, par, half = tile_at(i, ko)
                    if ko == 0:
                        act.wait_ge(v_done, TILES)
                    if ko <= AHEAD:
                        last = ((t + 1) * P - 1) // STEP_TOKENS
                        act.wait_ge(o_copied, last + 3)
                    if ko >= 2:
                        act.wait_ge(w_done, t - 1)
                    act.activation(OR[par][:, 0:P], QA[:, bass.ds(t * P, P)], ACT.Copy)
                    act.activation(OR[par][0:DB, P:2 * P], QB[0:DB, bass.ds(t * P, P)], ACT.Copy).then_inc(or_ready, 1)
                if kx is not None:
                    t, par, half = tile_at(i, kx)
                    act.wait_ge(xt1_done, t + 1)
                    if kx >= 2:
                        act.wait_ge(router_done, t - 1)
                    copy_xt(XT[par], bank[1]).then_inc(xt1_copied, 1)
                    copy_xt(XN2T[:, bass.ds(t * 2 * P, 2 * P)], bank[1]).then_inc(xn2t_saved, 1)

            def exp_logits(s):
                if s == TILES + 2:
                    act.wait_ge(log_shifted, 1)
                    act.activation(RT[:, 3 * TE:4 * TE], RT[:, 2 * TE:3 * TE], ACT.Exp).then_inc(log_exp, 1)

            mixer_lags = (0, 2, AHEAD + 1)

            def mixer_beside(s):
                if s >= MIXER_START - 1:
                    mixer_step(0, stages(s - MIXER_START + 1, mixer_lags, [TILES] * 3))

            act.sem_inc(o_copied, 2)
            two_by_two(act, patch_step, (1, 2, 4, SCORE_LAG, WEIGH_LAG), TILES,
                       counts=(TILES,) * 3 + (PAIR_STEPS,) * 2, after=mixer_beside)

            two_by_two(act, mixer_step, mixer_lags, TILES, exp_logits, start=PATCH_END - MIXER_START + 1)

            def copy_group(n, par):
                act.wait_ge(ffn_t_done, n + 1)
                copy_xt(XTF[par], bank[5]).then_inc(ffn_xt, 1)

            def group_step(i, ks):
                kx, kg = ks
                if kg is not None:
                    n, par, half = tile_at(i, kg)
                    gelu(TILES + n, par, True)
                if kx is not None and kx >= 2:
                    n, par, half = tile_at(i, kx)
                    act.wait_ge(f1_done, 2 * (TILES + n - 1))
                    copy_group(n, par)

            for n in range(2):
                copy_group(n, n)
            two_by_two(act, group_step, (0, 1), GROUPS)

        @block.vector
        def _(dve):
            def norm(dst, src, mv, rstd):
                return dve.tensor_scalar(dst, src, mv[:, 0:1], rstd, ALU.subtract, ALU.mult)

            for par in range(2):
                dve.memset(XT[par][DB:DB + 1, P:2 * P], 1.0).then_inc(set_up, 1)
            dve.wait_ge(h_set, 1)

            def attention_step(i, m, k_max, d, k_share):
                if k_share is not None:
                    p = tile_at(i, k_share)[0]
                    a = 2 * p + d
                    dve.wait_ge(exp_done, a + 1)
                    dve.reduce_sum(SM[0:K2, :], PR[d][0:K2, :].rearrange("p (m q) -> p m q", q=SEQ), axis=AX.X).then_inc(denom, 1)
                if k_max is not None:
                    b = 2 * tile_at(i, k_max)[0] + m
                    dve.wait_ge(scores_done, b + 1)
                    dve.reduce_max(MX[0:K2, :], bank[4 + m][0:K2, 0:NP2 * SEQ].rearrange("p (m q) -> p m q", q=SEQ), axis=AX.X).then_inc(max_ready, 1)
                if k_share is not None:
                    dve.wait_ge(denom, 3 * a + 1)
                    dve.reciprocal(RC[0:K2, :], SM[0:K2, :]).then_inc(denom, 1)
                if k_max is not None:
                    dve.wait_ge(max_ready, b + 1)
                    dve.tensor_tensor(SB[m][0:K2, :].rearrange("p (m q) -> p m q", q=SEQ),
                                      bank[4 + m][0:K2, 0:NP2 * SEQ].rearrange("p (m q) -> p m q", q=SEQ),
                                      MX[0:K2, :].unsqueeze(2).to_broadcast([K2, NP2, SEQ]), ALU.subtract).then_inc(s_shifted, 1)
                if k_share is not None:
                    dve.wait_ge(denom, 3 * a + 2)
                    dve.tensor_tensor(R2[0:K2, :].rearrange("p (m h) -> p m h", h=2),
                                      RC[0:K2, :].unsqueeze(2).to_broadcast([K2, NP2, 2]),
                                      const("parity", K2).unsqueeze(1).to_broadcast([K2, NP2, 2]), ALU.mult).then_inc(denom, 1)
                    dve.wait_ge(denom, 3 * a + 3)
                    dve.wait_ge(v2_in[d], 32 * (p + 1))
                    dve.tensor_tensor(VS[d][0:K2, :].rearrange("p (m d) -> p m d", d=HD),
                                      V2[d][0:K2, :].rearrange("p (m d) -> p m d", d=HD),
                                      R2[0:K2, :].unsqueeze(2).to_broadcast([K2, 2 * NP2, HD]), ALU.mult).then_inc(vs_ready, 1)

            def patch_step(i, ks):
                kh, kn, ks_, kq, k_max, k_share = ks
                if kn is not None:
                    t, par, half = tile_at(i, kn)
                    dve.wait_ge(h_rstd, t + 1)
                    if kn >= 2:
                        dve.wait_ge(xt_transposed, t - 1)
                        dve.wait_ge(h_plus_xn, t - 1)
                    norm(XN[par], H[:, bass.ds(t * D, D)], MVH[par], RSH[par][:, 0:1]).then_inc(xn_ready, 1)
                if kq is not None:
                    t, par, half = tile_at(i, kq)
                    dve.wait_ge(qk_rstd, t + 1)
                    dve.wait_ge(qkT_done, t + 1)
                    norm(QKN[par][:, 0:D], bank[2][:, 0:D], MVQK[par][:, 0:2], RSQK[par][:, 0:1])
                    norm(QKN[par][:, D:2 * D], bank[2][:, D:2 * D], MVQK[par][:, 2:4], RSQK[par][:, 1:2]).then_inc(qk_normed, 1)
                if kh == 4:
                    dve.wait_ge(consts_in, 16)
                    dve.wait_ge(gains_in, 64)
                    dve.tensor_scalar(GM[:, 0:HEADS_A], const("heads_a"), GAIN[:, 0:1], GAIN[:, 1:2], ALU.mult, ALU.mult)
                    dve.tensor_scalar(GM[0:DB, HEADS_A:HEADS], const("heads_b", DB), GAIN[0:DB, 2:3], GAIN[0:DB, 3:4],
                                      ALU.mult, ALU.mult).then_inc(gains_ready, 1)
                attention_step(i, 0, k_max, 1, k_share)
                if kh is not None:
                    t, par, half = tile_at(i, kh)
                    if kh in (2, 4, 6, 8):
                        dve.wait_ge(h_set, t // 2 + 1)
                    elif kh == 10:
                        dve.wait_ge(h_set, TILES // 2)
                    dve.wait_ge(conv_done, t + 1)
                    h = H[:, bass.ds(t * D, D)]
                    dve.tensor_tensor(h, bank[0][:, 0:D], h, ALU.add).then_inc(h_added, 1)
                    dve.wait_ge(h_added, t + 1)
                    ride(dve)
                    dve.bn_stats(STH[:, :], H[:, bass.ds(t * D, D)]).then_inc(h_stats, 1)
                    dve.wait_ge(h_stats, t + 1)
                    ride(dve)
                    dve.bn_aggr(MVH[par][:, :], STH[:, :]).then_inc(h_aggr, 1)
                attention_step(i, 1, k_max, 0, k_max)
                if ks_ is not None:
                    t, par, half = tile_at(i, ks_)
                    dve.wait_ge(qk_done, t + 1)
                    for j in range(2):
                        last = dve.bn_stats(STQK[:, 6 * j:6 * j + 6], bank[2][:, j * D:j * D + D])
                    last.then_inc(qk_stats, 1)
                    dve.wait_ge(qk_stats, t + 1)
                    ride(dve)
                    for j in range(2):
                        last = dve.bn_aggr(MVQK[par][:, 2 * j:2 * j + 2], STQK[:, 6 * j:6 * j + 6])
                    last.then_inc(qk_aggr, 1)

            def mixer_step(i, ks):
                kw, kl, kh = ks
                if kw == PATCH_END - MIXER_START:
                    dve.wait_ge(o_copied, STEPS + 2)
                    for par in range(2):
                        dve.memset(XTF[par][DB:DB + 1, P:2 * P], 1.0).then_inc(set_up, 1)
                if kw is not None:
                    t, par, half = tile_at(i, kw)
                    if kw in (0, 2):
                        dve.wait_ge(kr_ready, STEPS if kw else STEPS - 4)
                    dve.tensor_copy(XN2T[DB:DB + 1, bass.ds(t * 2 * P + P, P)], const("ones")[DB:DB + 1])
                    dve.wait_ge(w_done, t + 1)
                    h = H[:, bass.ds(t * D, D)]
                    dve.tensor_tensor(h, bank[0][:, 0:D], h, ALU.add).then_inc(h2_added, 1)
                    dve.wait_ge(h2_added, t + 1)
                    ride(dve)
                    dve.bn_stats(STH[:, :], h).then_inc(h2_stats, 1)
                    dve.wait_ge(h2_stats, t + 1)
                    ride(dve)
                    dve.bn_aggr(MVH[par][:, :], STH[:, :]).then_inc(h2_aggr, 1)
                if kl is not None:
                    t, par, half = tile_at(i, kl)
                    dve.wait_ge(router_done, t + 1)
                    dve.tensor_copy(LOG[:, bass.ds(t * EXPERTS, EXPERTS)], bank[2][:, 0:EXPERTS]).then_inc(log_copied, 1)
                if kw is not None:
                    t, par, half = tile_at(i, kw)
                    dve.wait_ge(h2_rstd, t + 1)
                    if kw >= 2:
                        dve.wait_ge(xt1_done, t - 1)
                        dve.wait_ge(xn2_saved, t - 1)
                    norm(XR[par], H[:, bass.ds(t * D, D)], MVH[par], RSH[par][:, 0:1]).then_inc(xn2_ready, 1)
                if kl == TILES - 1:
                    choose()
                if kh == TILES + 1 - AHEAD:
                    slots()
                    shares()
                    group_experts()
                if kh is not None:
                    t, par, half = tile_at(i, kh)
                    dve.wait_ge(y_done, t + 1)
                    dve.tensor_tensor(COMMON[:, :, bass.ds(t * (D // 2), D // 2)],
                                      bank[6 + par][:, 0:D].rearrange("p (g n) -> p g n", g=2),
                                      B2[:, 0:D].rearrange("p (g n) -> p g n", g=2), ALU.add).then_inc(y_used, 1)

            steps = [0]

            def then(ins):
                steps[0] += 1
                ins.then_inc(rt, 1)
                dve.wait_ge(rt, steps[0])

            def te(n):
                return RT[:, n * TE:n * TE + TE]

            def by_tile(ap):
                return ap.rearrange("p (t e) -> p t e", e=EXPERTS)

            def by_expert(ap):
                return ap.rearrange("p (e t) -> p e t", t=TILES)

            def over_e(ap):
                return ap.unsqueeze(2).to_broadcast([P, TILES, EXPERTS])

            def over_t(ap):
                return ap.unsqueeze(1).to_broadcast([P, TILES, EXPERTS])

            def small(n):
                return SMALL[:, n * TILES:n * TILES + TILES]

            def per_e(n):
                return SMALLE[:, n * EXPERTS:n * EXPERTS + EXPERTS]

            onehot, scratch, shifted, exped = te(0), te(1), te(2), te(3)
            top, total, prob, inverse, is0, keep, pick = (small(n) for n in range(7))
            counts, running, before = te(4), te(5), te(6)

            def choose():
                dve.wait_ge(log_copied, TILES)
                then(dve.reduce_max(top, by_tile(LOG[:, :]), axis=AX.X))
                dve.tensor_tensor(by_tile(shifted), by_tile(LOG[:, :]), over_e(top), ALU.subtract).then_inc(log_shifted, 1)
                then(dve.tensor_tensor(by_tile(scratch), by_tile(LOG[:, :]), over_e(top), ALU.is_equal))
                then(dve.tensor_tensor(by_tile(scratch), by_tile(scratch), over_t(const("first")), ALU.mult))
                then(dve.reduce_max(pick, by_tile(scratch), axis=AX.X))
                dve.tensor_tensor(by_tile(onehot), over_t(const("first")), over_e(pick), ALU.is_equal).then_inc(chosen, 1)

            def shares():
                dve.wait_ge(log_exp, 1)
                then(dve.reduce_sum(total, by_tile(exped), axis=AX.X))
                then(dve.reciprocal(prob, total))
                then(dve.reciprocal(inverse, prob))
                dve.tensor_copy(is0, by_tile(onehot)[:, :, 0])
                then(dve.tensor_tensor(inverse, prob, inverse, ALU.mult))
                then(dve.tensor_scalar(keep, prob, -1.0, 1.0, ALU.mult, ALU.add))
                then(dve.tensor_tensor(inverse, inverse, keep, ALU.subtract))
                then(dve.tensor_tensor(inverse, inverse, is0, ALU.mult))
                then(dve.tensor_tensor(KEEP1[:, :], keep, inverse, ALU.add))
                then(dve.tensor_tensor(inverse, prob, is0, ALU.mult))
                then(dve.tensor_tensor(SHARE[:, :], prob, inverse, ALU.subtract))
                dve.wait_ge(xn2_saved, TILES)
                for place, t0, t1 in ((XN2_EARLY, 0, EARLY_ROWS), (XN2_LATE, EARLY_ROWS, TILES)):
                    rows = place.rearrange("p (t w) -> p t w", w=ROW)
                    dve.tensor_copy(rows[:, :, D], SHARE[:, t0:t1])
                    last = dve.tensor_copy(rows[:, :, D + 1].bitcast(I32), IDS[:, t0:t1])
                last.then_inc(rows_tagged, 1)

            def slots():
                dve.wait_ge(ranks_done, 1)
                then(dve.tensor_copy(by_expert(counts), bank[2][:, 0:TE].rearrange("p (t e) -> p e t", e=EXPERTS)))
                then(dve.tensor_tensor_scan(running, const("keep"), counts, 0.0, ALU.mult, ALU.add))
                then(dve.tensor_tensor(before, running, counts, ALU.subtract))
                then(dve.tensor_tensor(by_expert(scratch), by_expert(running)[:, :, TILES - 1].unsqueeze(2).to_broadcast([P, EXPERTS, TILES]),
                                       const("thresholds").unsqueeze(1).to_broadcast([P, EXPERTS, TILES]), ALU.is_gt))
                then(dve.reduce_sum(per_e(0), by_expert(scratch), axis=AX.X))
                then(dve.memset(per_e(0)[:, 0:1], 0.0))
                then(dve.tensor_tensor_scan(per_e(1), const("ones")[:, 0:EXPERTS], per_e(0), 0.0, ALU.mult, ALU.add))
                then(dve.tensor_tensor(per_e(2), per_e(1), per_e(0), ALU.subtract))
                then(dve.tensor_scalar(per_e(3), per_e(2), float(P), None, ALU.mult))
                then(dve.tensor_tensor(by_expert(before), by_expert(before), per_e(3).unsqueeze(2).to_broadcast([P, EXPERTS, TILES]), ALU.add))
                then(dve.tensor_tensor(by_tile(scratch), bank[0][:, 0:TE].rearrange("p (t e) -> p t e", e=EXPERTS),
                                       before.rearrange("p (e t) -> p t e", t=TILES), ALU.add))
                then(dve.tensor_tensor(scratch, scratch, onehot, ALU.mult))
                then(dve.reduce_sum(top, by_tile(scratch), axis=AX.X))
                then(dve.tensor_scalar(pick, by_tile(onehot)[:, :, 0], float(GROUPS * P), None, ALU.mult))
                then(dve.tensor_tensor(top, top, pick, ALU.add))
                dve.tensor_copy(SLOT[:, :], top).then_inc(slots_ready, 1)

            def group_experts():
                cmp = GCMP[0:1, :].rearrange("p (g e) -> p g e", e=EXPERTS)
                then(dve.tensor_tensor(cmp, per_e(1)[0:1, :].unsqueeze(1).to_broadcast([1, GROUPS, EXPERTS]),
                                       const("groups", 1).unsqueeze(2).to_broadcast([1, GROUPS, EXPERTS]), ALU.is_le))
                then(dve.reduce_sum(SMALL[0:1, 8 * TILES:8 * TILES + GROUPS], cmp, axis=AX.X))
                dve.tensor_scalar(GROUP_EXPERT[0:1, :], SMALL[0:1, 8 * TILES:8 * TILES + GROUPS], float(EXPERTS - 1), None,
                                  ALU.min).then_inc(groups_ready, 1)

            def copy_w1(n, par, guard):
                expert = dve.value_load(GROUP_EXPERT[0:1, bass.ds(n, 1)], min_val=0, max_val=EXPERTS - 1)
                if guard:
                    dve.wait_ge(f1_done, 2 * (TILES + n - 1))
                cols = bass.ds(expert * DFF, DFF)
                dve.tensor_copy(W1R[par][:, 0:DFF], W1A[:, cols])
                dve.tensor_copy(W1R[par][0:DB + 1, DFF:2 * DFF], W1B[0:DB + 1, cols]).then_inc(w1_copied, 1)

            def base(t):
                if t >= 4:
                    dve.wait_ge(out_stored[t % 4], 16 * (t // 4))
                dve.scalar_tensor_tensor(out=BASE[t % 4].rearrange("p (g n) -> p g n", g=2),
                                         in0=COMMON[:, :, t * (D // 2):(t + 1) * (D // 2)], scalar=KEEP1[:, t:t + 1],
                                         in1=H[:, t * D:t * D + D].rearrange("p (g n) -> p g n", g=2),
                                         op0=ALU.mult, op1=ALU.add).then_inc(base_ready, 1)

            def after_routing(s):
                if s == TILES + AHEAD - 2:
                    dve.wait_ge(groups_ready, 1)
                    dve.wait_ge(scattered, 16 * TILES)
                    for n in range(2):
                        copy_w1(n, n, False)
                if s >= TILES + 4:
                    saved = s - AHEAD
                    dve.wait_ge(y_used, saved)
                    first = 4 * (s - TILES - 4) if s < TILES + 8 else saved - 1
                    for t in range(first, min(first + 4, saved)):
                        base(t)

            mixer_lags = (0, 2, AHEAD + 1)

            def mixer_beside(s):
                if s == MIXER_START - 1:
                    dve.wait_ge(v_done, TILES)
                    for par in range(2):
                        dve.memset(OR[par][DB:DB + 1, P:2 * P], 1.0).then_inc(set_up, 1)
                    dve.wait_ge(h_plus_xn, TILES)
                if s >= MIXER_START:
                    mixer_step(0, stages(s - MIXER_START, mixer_lags, [TILES] * 3))

            two_by_two(dve, patch_step, (0, 1, 2, 3, SCORE_LAG, WEIGH_LAG), TILES,
                       counts=(TILES,) * 4 + (PAIR_STEPS,) * 2, after=mixer_beside)

            dve.wait_ge(mixer_w_in, 16 * 5)
            two_by_two(dve, mixer_step, mixer_lags, TILES, after_routing, start=PATCH_END - MIXER_START)

            def group_step(i, ks):
                kw, kh = ks
                if kw is not None:
                    n, par, half = tile_at(i, kw)
                    copy_w1(n, par, True)
                if kh is not None:
                    n, par, half = tile_at(i, kh)
                    expert = dve.value_load(GROUP_EXPERT[0:1, bass.ds(n, 1)], min_val=0, max_val=EXPERTS - 1)
                    dve.wait_ge(y_done, TILES + n + 1)
                    if kh >= 2:
                        dve.wait_ge(y_added[par], 16 * half)
                    dve.tensor_tensor(YR[par], bank[6 + par][:, 0:D], B2[:, bass.ds(expert * D, D)], ALU.add).then_inc(y_used, 1)
                    dve.wait_ge(y_used, TILES + n + 1)
                    if kh == 0:
                        dve.wait_ge(slot_rows_in, 16)
                    dve.tensor_scalar(YR[par], YR[par], SLOT_ROWS[:, bass.ds(n * 2, 1)], None, ALU.mult).then_inc(y_scaled, 1)

            two_by_two(dve, group_step, (0, 2), GROUPS, start=2)

        @block.gpsimd
        def _(pool):
            pool.memset(NEGHALF[:, :], -0.5).then_inc(zeroed, 1)
            def add_bias(t0, t1):
                h = H[:, t0 * D:t1 * D].rearrange("p (t d) -> p t d", d=D)
                pool.tensor_tensor(h, h, CB[:, :].unsqueeze(1).to_broadcast([P, t1 - t0, D]), ALU.add).then_inc(h_set, 1)

            pool.wait_ge(pos_in[0], 32)
            add_bias(0, 2)

            def spread(p, par, k):
                a = 2 * p + par
                if k >= 1:
                    pool.wait_ge(scores_done, a - 1)
                width = HEADS_A * SEQ
                for n in range(STEP_IMAGES):
                    pool.tensor_tensor(KR[par][:, n * width:(n + 1) * width].rearrange("p (h q) -> p h q", q=SEQ),
                                       KA[:, bass.ds(a * STEP_TOKENS + n * SEQ, SEQ)].unsqueeze(1).to_broadcast([P, HEADS_A, SEQ]),
                                       GM[:, 0:HEADS_A].unsqueeze(2).to_broadcast([P, HEADS_A, SEQ]), ALU.mult)
                base, hb = STEP_IMAGES * width, HEADS - HEADS_A
                for n in range(STEP_IMAGES):
                    last = pool.tensor_tensor(KR[par][0:DB, base + n * hb * SEQ:base + (n + 1) * hb * SEQ].rearrange("p (h q) -> p h q", q=SEQ),
                                              KB[0:DB, bass.ds(a * STEP_TOKENS + n * SEQ, SEQ)].unsqueeze(1).to_broadcast([DB, hb, SEQ]),
                                              GM[0:DB, HEADS_A:HEADS].unsqueeze(2).to_broadcast([DB, hb, SEQ]), ALU.mult)
                last.then_inc(kr_ready, 1)

            def tiles_of(p, par):
                return -(-(2 * p + par + 1) * STEP_TOKENS // P)

            in_loop = range(2, TILES - SPREAD_LAG)

            def k_tiles(p, par):
                if isinstance(p, int):
                    return tiles_of(p, par)
                return p + max(tiles_of(q, par) - q for q in in_loop)

            def patch_step(i, ks):
                kh, kq, kx, k_spread = ks
                if kx is not None:
                    t, par, half = tile_at(i, kx)
                    pool.wait_ge(xn_ready, t + 1)
                    h = H[:, bass.ds(t * D, D)]
                    pool.tensor_tensor(h, h, XN[par], ALU.add).then_inc(h_plus_xn, 1)
                if k_spread is not None:
                    p = tile_at(i, k_spread)[0]
                    if k_spread == 0:
                        pool.wait_ge(gains_ready, 1)
                    pool.wait_ge(qkT_copied, k_tiles(p, 0))
                    spread(p, 0, k_spread)
                if kh is not None:
                    t, par, half = tile_at(i, kh)
                    if kh >= 1:
                        pool.wait_ge(h_rstd, t)
                    pool.wait_ge(h_aggr, t + 1)
                    ride(pool)
                    pool.tensor_scalar(VE[:, 0:1], MVH[par][:, 1:2], EPS, None, ALU.add).then_inc(ve_h, 1)
                    pool.wait_ge(ve_h, t + 1)
                    pool.tensor_tensor(RSH[par][:, :], VE[:, 0:1], NEGHALF[:, 0:1], ALU.pow).then_inc(h_rstd, 1)
                if k_spread is not None:
                    p = tile_at(i, k_spread)[0]
                    pool.wait_ge(qkT_copied, k_tiles(p, 1))
                    spread(p, 1, k_spread)
                if kq is not None:
                    t, par, half = tile_at(i, kq)
                    if kq >= 1:
                        pool.wait_ge(qk_rstd, t)
                    pool.wait_ge(qk_aggr, t + 1)
                    ride(pool)
                    pool.tensor_scalar(VE[:, 1:3], MVQK[par].rearrange("p (j s) -> p j s", s=2)[:, :, 1], EPS, None, ALU.add).then_inc(ve_qk, 1)
                    pool.wait_ge(ve_qk, t + 1)
                    pool.tensor_tensor(RSQK[par][:, :], VE[:, 1:3], NEGHALF[:, 0:2], ALU.pow).then_inc(qk_rstd, 1)
                if kh is not None and kh <= 7:
                    t = 2 * kh + 2
                    for part in (1, 2):
                        if t == ROW_PARTS[part][0]:
                            pool.wait_ge(pos_in[part], 16)
                    add_bias(t, t + 2)

            def zero_packed():
                zeros = RINGS[:, 4 * DFF - ROW:4 * DFF]
                pool.wait_ge(o_copied, STEPS + 2)
                pool.memset(zeros[:, 0:D + 1], 0.0).then_inc(zeroed, 1)
                pool.memset(zeros[:, D + 1:ROW].bitcast(I32), TOKENS).then_inc(zeroed, 1)
                pool.wait_ge(zeroed, 3)
                pool.dma_start(packed.rearrange("(g p) d -> p g d", p=P),
                               zeros.unsqueeze(1).to_broadcast([P, GROUPS, ROW])).then_inc(packed_zeroed, 16)

            def mixer_step(i, ks):
                kh, = ks
                if kh is not None:
                    t, par, half = tile_at(i, kh)
                    if kh >= 1:
                        pool.wait_ge(h2_rstd, t)
                    pool.wait_ge(h2_aggr, t + 1)
                    ride(pool)
                    pool.tensor_scalar(VE[:, 0:1], MVH[par][:, 1:2], EPS, None, ALU.add).then_inc(ve_h, 1)
                    pool.wait_ge(ve_h, TILES + t + 1)
                    pool.tensor_tensor(RSH[par][:, :], VE[:, 0:1], NEGHALF[:, 0:1], ALU.pow).then_inc(h2_rstd, 1)
                    pool.wait_ge(xn2_ready, t + 1)
                    if kh == EARLY_ROWS:
                        zero_packed()
                    rows = xn2_rows(t)[:, 0:D] if isinstance(t, int) else XN2_LATE[:, bass.ds((t - EARLY_ROWS) * ROW, D)]
                    pool.tensor_copy(rows, XR[par]).then_inc(xn2_saved, 1)

            mixer_lags = (0,)

            def mixer_beside(s):
                if s >= MIXER_START:
                    mixer_step(0, stages(s - MIXER_START, mixer_lags, [TILES]))

            two_by_two(pool, patch_step, (0, 2, 1, SPREAD_LAG), TILES, counts=(TILES,) * 3 + (PAIR_STEPS,),
                       after=mixer_beside)
            two_by_two(pool, mixer_step, mixer_lags, TILES, start=SPREAD_LAG + PAIR_STEPS - MIXER_START,
                       outside=EARLY_ROWS + 1)

            pool.wait_ge(packed_zeroed, 16)
            pool.wait_ge(slots_ready, 1)
            pool.wait_ge(rows_tagged, 1)
            for t in range(TILES):
                pool.indirect_dma_start(packed, bass.IndirectOffsetOnAxis(ap=SLOT[:, t:t + 1], axis=0),
                                        xn2_rows(t), None,
                                        bounds_check=GROUPS * P - 1, oob_is_err=False).then_inc(scattered, 16)

            def group_step(i, ks):
                kh, = ks
                n, par, half = tile_at(i, kh)
                if kh >= 2:
                    pool.wait_ge(y_added[par], 16 * half)
                pool.tensor_copy(ID[par][:, :], SLOT_ROWS[:, bass.ds(2 * n + 1, 1)].bitcast(I32)).then_inc(id_ready, 1)
                pool.wait_ge(id_ready, n + 1)
                pool.wait_ge(y_scaled, n + 1)
                if kh >= 1:
                    pool.wait_ge(y_added[1 - par], 16 * (half + par))
                ride(pool)
                pool.indirect_dma_start(out, bass.IndirectOffsetOnAxis(ap=ID[par][:, 0:1], axis=0), YR[par], None,
                                        bounds_check=TOKENS - 1, oob_is_err=False,
                                        compute_op=ALU.add).then_inc(y_added[par], 16)

            pool.wait_ge(slot_rows_in, 16)
            for ring4 in range(4):
                pool.wait_ge(out_stored[ring4], 16 * len(range(ring4, TILES, 4)))
            two_by_two(pool, group_step, (0,), GROUPS)


def _consts(np):
    c = np.zeros((P, NCONST), np.float32)

    def put(name, value):
        a, b = CONSTS[name]
        c[:, a:b] = value

    put("ident", np.eye(P))
    put("before", np.triu(np.ones((P, P)), 1))
    put("ones", 1.0)
    put("first", np.arange(EXPERTS, 0, -1))
    put("thresholds", np.arange(TILES) * P)
    put("groups", np.arange(GROUPS))
    put("keep", np.tile(np.arange(TILES) > 0, EXPERTS))
    row = np.arange(P)[:, None]
    put("heads_a", row // HD == np.arange(HEADS_A))
    put("heads_b", row // HD == np.arange(HEADS - HEADS_A))
    put("parity", row // SEQ == np.arange(2))
    return c


def _position_rows(np):
    edges = np.arange(1.0 / POS_TABLE_SIDE, 1.0, 1.0 / POS_TABLE_SIDE, dtype=np.float32)
    at = np.searchsorted(edges, np.arange(0.0, 1.0 - 1e-06, 1.0 / GRID, dtype=np.float32), side="right")
    return (at[:, None] * POS_TABLE_SIDE + at).reshape(-1)


def kernel(**inputs):
    import numpy as np
    import concourse.bacc as _bacc
    from concourse.bass_utils import run_bass_kernel_spmd as _run

    g = {k: np.asarray(v) for k, v in inputs.items()}

    def with_row(w, b):
        return np.concatenate([w, b[None]], axis=0)

    x = g["x"].reshape(IMAGES, CHANNELS, GRID, PATCH, GRID, PATCH).transpose(1, 3, 5, 0, 2, 4)
    x = x.reshape(KC, P, TILES, P).transpose(2, 1, 0, 3).reshape(TILES, P, KC * P)
    zero = np.zeros((D,), np.float32)
    w_k = with_row(g["L0_attn_Wk"].T, g["L0_attn_bk"])
    w_qkv = np.concatenate([with_row(g["L0_attn_Wq"].T, zero), w_k[:, P:D], w_k[:, 0:P],
                            with_row(g["L0_attn_Wv"].T, g["L0_attn_bv"])], axis=1)
    pos = g["L0_tok_pos_table"][_position_rows(np)]
    pos = np.tile(pos, (IMAGES, 1)).reshape(TILES, P, D).transpose(1, 0, 2).reshape(P, TILES * D)
    w1 = g["L0_ffn_W1"].transpose(1, 0, 2).reshape(D, EXPERTS * DFF)
    arrays = {
        "patches": x,
        "conv_w": g["L0_tok_conv_w"].reshape(D, KC, P).transpose(2, 1, 0).reshape(P, KC * D),
        "conv_b": np.tile(g["L0_tok_conv_b"], (P, 1)),
        "pos": pos,
        "w_qkv": w_qkv,
        "w_o": with_row(g["L0_attn_Wo"].T, g["L0_attn_bo"]),
        "gq": g["L0_attn_gq"][:, None],
        "gk": g["L0_attn_gk"][:, None],
        "w_router": with_row(g["L0_ffn_Ws"], g["L0_ffn_bs"]),
        "w1": w1[0:P],
        "w1_rest": with_row(w1[P:D], g["L0_ffn_b1"].reshape(-1)),
        "w2": g["L0_ffn_W2"].reshape(EXPERTS, FC, P, D).transpose(2, 0, 1, 3).reshape(P, EXPERTS * FC * D),
        "b2": np.tile(g["L0_ffn_b2"].reshape(1, -1), (P, 1)),
        "consts": _consts(np),
        "ids": np.arange(TOKENS, dtype=np.int32).reshape(TILES, P).T,
    }
    arrays = {f"in_{k}": np.ascontiguousarray(v) for k, v in arrays.items()}
    nc = _bacc.Bacc("TRN2", target_bir_lowering=False, num_devices=1)
    args = [nc.dram_tensor(k, v.shape, mybir.dt.from_np(v.dtype), kind="ExternalInput").ap() for k, v in arrays.items()]
    out = nc.dram_tensor("out", (TOKENS, D), F32, kind="ExternalOutput").ap()
    vit_kernel(nc, *args, out)
    r = _run(nc, [arrays], core_ids=[0])
    return r.results[0]["out"].reshape(IMAGES, SEQ, D)
```
